# Optimizing a Trainium2 kernel written in Bass

```python
import numpy as np
import jax
import jax.numpy as jnp

def _softmax(x, axis=-1):
    return jax.nn.softmax(x, axis=axis)

def _gelu(x):
    return jax.nn.gelu(x, approximate=True)

def _silu(x):
    return jax.nn.silu(x)

def _sigmoid(x):
    return jax.nn.sigmoid(x)

def _layernorm(x, axis=-1, eps=1e-05):
    m = jnp.mean(x, axis=axis, keepdims=True)
    v = jnp.var(x, axis=axis, keepdims=True)
    return (x - m) / jnp.sqrt(v + eps)

def _scatter_add(tgt, idx, src, axis=0):
    return tgt.at[idx].add(src)

def _segment_sum(src, seg, n):
    return jax.ops.segment_sum(src, seg, n)
kernel_name = 'mk_gnn_preln_d1_gnn_r8_6da32f'

def setup_inputs(seed: int=0):
    np.random.seed(seed)
    _w = jnp.asarray

    def _rec_inputs():
        import jax
        import jax.numpy as jnp
        _gk = jax.random.key(seed)
        x = -0.0003713 + 1 * jax.random.normal(jax.random.fold_in(_gk, 1), (6250, 256), jnp.float32)
        _s = jax.random.randint(jax.random.fold_in(_gk, 2), (50000,), 0, 6250, jnp.int32)
        _d = jax.random.randint(jax.random.fold_in(_gk, 3), (50000,), 0, 6250, jnp.int32)
        _loop = jnp.arange(6250, dtype=jnp.int32)
        src = jnp.concatenate([_s, _d, _loop])
        dst = jnp.concatenate([_d, _s, _loop])
        _o = jnp.argsort(dst, stable=True)
        src = src[_o]
        dst = dst[_o]
        edge_attr_2 = -0.000414295 + 0.999828 * jax.random.normal(jax.random.fold_in(_gk, 12), (106250, 2), jnp.float32)
        node_vec1 = jax.random.uniform(jax.random.fold_in(_gk, 13), (6250, 1), jnp.float32, 0.0, 0.999957)
        return (x, src, dst, edge_attr_2, node_vec1)
    x, src, dst, edge_attr_2, node_vec1 = _rec_inputs()

    def _L0_gnn_setup():
        import jax, jax.numpy as jnp
        import numpy as np
        N_NODES = 6250
        N_EDGES = 100000
        D = 256
        EPS = 1e-08
        BN_EPS = 1e-05
        key = jax.random.key(seed)
        ks = jax.random.split(key, 11)
        return {'h': jax.random.normal(ks[0], (N_NODES, D), jnp.float32), 'eig': jax.random.normal(ks[1], (N_EDGES, 2), jnp.float32), 'snorm_n': jax.random.uniform(ks[2], (N_NODES, 1), jnp.float32), 'W1': jax.random.normal(ks[3], (2 * D, D), jnp.float32) * (1.0 / np.sqrt(2 * D)), 'b1': jnp.zeros((D,), jnp.float32), 'W2': jax.random.normal(ks[4], (4 * D, D), jnp.float32) * (1.0 / np.sqrt(4 * D)), 'b2': jnp.zeros((D,), jnp.float32), 'gamma': jnp.ones((D,), jnp.float32), 'beta': jnp.zeros((D,), jnp.float32), 'src': jax.random.randint(ks[5], (N_EDGES,), 0, N_NODES, jnp.int64 if jax.config.jax_enable_x64 else jnp.int32), 'dst': jax.random.randint(ks[6], (N_EDGES,), 0, N_NODES, jnp.int64 if jax.config.jax_enable_x64 else jnp.int32)}
    _L0_gnn_all = _L0_gnn_setup()
    _L0_gnn_in = {k: v for k, v in _L0_gnn_all.items() if k in ('W1', 'b1', 'W2', 'b2', 'gamma', 'beta')}
    del _L0_gnn_all
    return {'x': x, 'src': src, 'dst': dst, 'edge_attr_2': edge_attr_2, 'node_vec1': node_vec1, 'L0_gnn_W1': _L0_gnn_in['W1'], 'L0_gnn_b1': _L0_gnn_in['b1'], 'L0_gnn_W2': _L0_gnn_in['W2'], 'L0_gnn_b2': _L0_gnn_in['b2'], 'L0_gnn_gamma': _L0_gnn_in['gamma'], 'L0_gnn_beta': _L0_gnn_in['beta']}

def reference(x, src, dst, edge_attr_2, node_vec1, L0_gnn_W1, L0_gnn_b1, L0_gnn_W2, L0_gnn_b2, L0_gnn_gamma, L0_gnn_beta):
    import jax
    import jax.numpy as jnp

    def _L0_gnn_ref(h, eig, snorm_n, W1, b1, W2, b2, gamma, beta, src, dst):
        import jax, jax.numpy as jnp
        import numpy as np
        N_NODES = 6250
        N_EDGES = 100000
        D = 256
        EPS = 1e-08
        BN_EPS = 1e-05
        n = h.shape[0]
        seg = lambda x: jax.ops.segment_sum(x, dst, num_segments=n)
        z2 = jnp.concatenate([h[src], h[dst]], axis=1)
        e = z2 @ W1 + b1
        deg = seg(jnp.ones((dst.shape[0],), h.dtype))
        mean_agg = seg(e) / jnp.maximum(deg, 1.0)[:, None]
        w = eig[:, 0]
        s = seg(jnp.abs(w)) + EPS
        wn = w / s[dst]
        dir_av = seg(e * jnp.abs(wn)[:, None])
        dir_dx = jnp.abs(seg(e * wn[:, None]) - h)
        hc = jnp.concatenate([h, mean_agg, dir_av, dir_dx], axis=1)
        out = hc @ W2 + b2
        out = out * snorm_n
        mu = out.mean(axis=0)
        var = jnp.mean((out - mu) ** 2, axis=0)
        out = (out - mu) / jnp.sqrt(var + BN_EPS) * gamma + beta
        out = jax.nn.relu(out)
        out = h + out
        return out
    h = jnp.maximum(_layernorm(x, axis=-1), 0.0)
    x = x + _L0_gnn_ref(h, edge_attr_2, node_vec1, L0_gnn_W1, L0_gnn_b1, L0_gnn_W2, L0_gnn_b2, L0_gnn_gamma, L0_gnn_beta, src, dst)
    return x

_drawn_inputs = setup_inputs


def setup_inputs(seed=0):
    import zlib

    import numpy as np

    out = dict(_drawn_inputs(seed))
    spreads = {'L0_gnn_b1': (0.0, 0.292),
     'L0_gnn_b2': (0.0, 0.1),
     'L0_gnn_gamma': (1.0, 0.2),
     'L0_gnn_beta': (0.0, 0.1)}
    factors = {}
    for name, (base, spread) in spreads.items():
        noise = np.random.default_rng([zlib.crc32(name.encode()), seed]).standard_normal(out[name].shape)
        drawn = base * np.exp(spread * noise) if base else spread * noise
        out[name] = jnp.asarray(drawn.astype(out[name].dtype))
    for name, factor in factors.items():
        out[name] = (out[name] * factor).astype(out[name].dtype)
    return out
```

```python
from contextlib import ExitStack

import concourse.bass as bass
from concourse import mybir

F32 = mybir.dt.float32
I32 = mybir.dt.int32
U32 = mybir.dt.uint32
ALU = mybir.AluOpType
ACT = mybir.ActivationFunctionType
AX_X = mybir.AxisListType.X

P = 128
D = 256
HALVES = D // P
SUMS = 3
TILES = 3
WINDOW = 32
GROUPS = 6
RING = 3
HALF = GROUPS // 2
WORDS = 6
SRC, DST, REL, ONE = 0, 1, 2, 3
LAG = 2
SUPER = 4
SEL = SUMS * WINDOW
LN_EPS = 1e-5
BN_EPS = 1e-5
SUM_EPS = 1e-8


def build(nc, x, src, dst, eig, snorm, W1, b1, W2, b2, gamma, beta, out):
    N = x.shape[0]
    E = src.shape[0]
    tiles = -(-E // P)
    groups = -(-tiles // TILES)
    slots = groups * TILES
    iters, rest = divmod(groups, GROUPS)
    NB = -(-N // iters)
    last_nb = N - (iters - 1) * NB
    full, tail_rows = divmod(N, P)
    supers = full // SUPER
    pairs = supers // 2
    rounds = -(-N // P)
    NP = -(-max(N + WINDOW, rounds * P) // 16) * 16
    rows_in = -(-slots // P)
    full_rb, rest_rows = divmod(E // P, P)
    tail_edges = E % P
    assert full % (2 * SUPER) == 0 and pairs >= 1 and 0 < tail_rows and iters > LAG and 0 < last_nb
    assert rows_in == full_rb + 1 and groups <= 512 and HALVES * NB <= 512 and slots * WORDS <= NP

    h_t_dram = nc.dram_tensor("h_t", [HALVES, P, (full + 1) * P], F32).ap()
    a_dram = nc.dram_tensor("a_rows", [N, D], F32).ap()
    xh_dram = nc.dram_tensor("x_plus_h", [N, D], F32).ap()
    rec_dram = nc.dram_tensor("edge_records", [P, slots, WORDS], F32).ap()

    ctx = ExitStack()
    with ctx:
        def sb(name, shape, dt=F32):
            return ctx.enter_context(nc.sbuf_tensor(name, shape, dt))

        def sem(name):
            return ctx.enter_context(nc.semaphore(name))

        def sems(name, n):
            return [sem(f"{name}{k}") for k in range(n)]

        table = sb("table", [P, SUMS, HALVES, NP])
        sums = sb("sums", [P, NP])
        ring = sb("ring", [P, RING * TILES, D])
        w1b = sb("w1b", [P, HALVES, D])
        w2 = sb("w2", [P, 4 * HALVES, D])
        ident = sb("ident", [P, P])
        ones = sb("ones", [P, P])
        pick = sb("pick", [P, SUMS, P])
        nodes_iota = sb("nodes_iota", [P, WINDOW])
        eps = sb("eps", [P, 1])
        b1_t = sb("b1_t", [P, HALVES])
        b2_t = sb("b2_t", [P, HALVES])
        gamma_t = sb("gamma_t", [P, HALVES])
        beta_t = sb("beta_t", [P, HALVES])
        rec = sb("rec", [P, 2, HALF * TILES, WORDS])
        sel = sb("sel", [P, 2, TILES, SUMS, WINDOW])
        b_rows = sb("b_rows", [P, HALVES, NB])
        h_blk = sb("h_blk", [P, HALVES, NB])
        val = sb("val", [P, SUMS, HALVES, NB])
        inv_deg = sb("inv_deg", [P, NB])
        inv_abs = sb("inv_abs", [P, NB])
        sn = sb("sn", [P, NB])
        sn_row = sb("sn_row", [1, NB])
        bn = sb("bn", [P, HALVES, iters, 6])
        bases = sb("bases", [1, iters + 1, 8], I32)
        small = sb("small", [P, 64])
        flag = sb("flag", [P, 1], I32)

        lnb = sums[:, 0:6 * SUPER * D].rearrange("p (k c n) -> p k c n", k=6, c=SUPER)
        x_sb = [lnb[:, k] for k in (0, 1)]
        h_sb = [lnb[:, k] for k in (2, 3)]
        ht_sb = [lnb[:, k].rearrange("p c n -> p (c n)").rearrange("p (h n) -> p h n", h=HALVES) for k in (4, 5)]
        a_sb = [ring[:, SUPER * k:SUPER * k + SUPER, :] for k in (0, 1)]
        w1a = val[:, :, :, :].rearrange("p v h n -> p (v h n)")[:, 0:HALVES * D].rearrange("p (h n) -> p h n", h=HALVES)
        plane = [table[:, v, h, :] for v in range(SUMS) for h in range(HALVES)]
        raw = plane[3]
        raw_n = rows_in * P
        raw_i = [raw[:, k * raw_n:(k + 1) * raw_n].bitcast(I32).rearrange("p (r e) -> p r e", r=rows_in) for k in (0, 1)]
        raw_f = [raw[:, k * raw_n:(k + 1) * raw_n].rearrange("p (r e) -> p r e", r=rows_in) for k in (2, 3, 4)]
        mask = [plane[4][:, k * slots:(k + 1) * slots] for k in range(3)]
        eig_sb = plane[4][:, 3 * slots:3 * slots + 2 * raw_n].rearrange("p (r e) -> p r e", r=rows_in)
        thr_i = plane[4][:, 3 * slots + 2 * raw_n:3 * slots + 2 * raw_n + groups].bitcast(I32)
        iota_i = plane[4][:, 3 * slots + 2 * raw_n + groups:3 * slots + 2 * raw_n + groups + WINDOW].bitcast(I32)
        assert 3 * slots + 2 * raw_n + groups + WINDOW <= NP and 5 * raw_n <= NP
        recs = plane[5][:, 0:slots * WORDS].rearrange("p (t k) -> p t k", k=WORDS)
        fin_x = [lnb[:, k] for k in (0, 1)]
        fin_y = [lnb[:, k].rearrange("p c n -> p (c n)").rearrange("p (h n) -> p h n", h=HALVES) for k in (2, 3)]
        out_t = [table[:, 0, h, :] for h in range(HALVES)]
        mv = [small[:, 8 * u:8 * u + 8].rearrange("p (c k) -> p c k", k=2) for u in (0, 1)]
        std = [small[:, 16 + 4 * u:20 + 4 * u] for u in (0, 1)]
        rstd = [small[:, 24 + 4 * u:28 + 4 * u] for u in (0, 1)]
        shift = [small[:, 32 + 4 * u:36 + 4 * u] for u in (0, 1)]
        count = small[:, 40:42]
        vote = small[:, 42:43]
        ok = small[:, 43:44]
        ok_less_1 = small[:, 44:45]
        bn_mv = small[:, 46:50].rearrange("p (h k) -> p h k", h=HALVES)
        bn_std = small[:, 50:52]
        bn_scale = small[:, 52:54]
        bn_shift = small[:, 54:56]
        stats6 = sb("stats6", [P, SUPER, 6])
        gen_rows = ring[:, 0, :]
        gen_sel = ring[:, 1:3, :].rearrange("p a n -> p (a n)")[:, 0:SUMS * P].rearrange("p (v n) -> p v n", v=SUMS)
        gen_nodes = ring[:, 3, 0:P]
        gen_rec = rec[:, 0, 0, :]

        bank = [ctx.enter_context(nc.psum_tensor(f"bank{k}", [P, 512], F32)) for k in range(8)]
        group_ps = [bank[0], bank[1]]
        b_ps = bank[2][:, 0:HALVES * NB].rearrange("p (h n) -> p h n", h=HALVES)
        deg_bc = bank[3][:, 0:NB]
        abs_bc = bank[3][:, NB:2 * NB]
        w_bc = bank[4][:, 0:NB]
        sn_bc = bank[4][:, NB:2 * NB]
        out_ps = bank[5][:, 0:HALVES * NB].rearrange("p (h n) -> p h n", h=HALVES)
        t_ps = [bank[4 + p][:, :].rearrange("p (c h n) -> p c h n", c=2, h=HALVES) for p in (0, 1)]
        a_ps = [bank[6 + p][:, :].rearrange("p (c n) -> p c n", c=2) for p in (0, 1)]

        waits_carried = sem("waits_carried")
        small_loaded = sem("small_loaded")
        w_loaded = sem("w_loaded")
        edges_cleared = sem("edges_cleared")
        edges_loaded = sem("edges_loaded")
        consts = sem("consts")
        picked = sem("picked")
        edges_float = sem("edges_float")
        edges_turned = sem("edges_turned")
        edges_copied = sem("edges_copied")
        base_spread = sem("base_spread")
        prep = sem("prep")
        voted = sem("voted")
        vote_sum = sem("vote_sum")
        recs_ready = sem("recs_ready")
        recs_stored = sem("recs_stored")
        flag_ready = sem("flag_ready")
        thresholds = sem("thresholds")
        zeroed = sem("zeroed")
        zeroed2 = sem("zeroed2")
        sums_zeroed = sem("sums_zeroed")
        x_loaded = sems("x_loaded", 2)
        ln_steps = sem("ln_steps")
        var_ready = sem("var_ready")
        std_ready = sem("std_ready")
        scale_ready = sem("scale_ready")
        h_ready = sems("h_ready", 2)
        xh_ready = sems("xh_ready", 2)
        xh_stored = sems("xh_stored", 2)
        h_turned = [sems(f"h_turned{u}_", 2) for u in (0, 1)]
        ht_copied = [sems(f"ht_copied{u}_", 2) for u in (0, 1)]
        ht_stored = sems("ht_stored", 2)
        a_done = [sems(f"a_done{u}_", 2) for u in (0, 1)]
        a_copied = [sems(f"a_copied{u}_", 2) for u in (0, 1)]
        a_stored = sems("a_stored", 2)
        gen_loaded = sem("gen_loaded")
        gen_gathered = sem("gen_gathered")
        gen_steps = sem("gen_steps")
        gen_sel_ready = sem("gen_sel_ready")
        gen_summed = sem("gen_summed")
        gen_added = sem("gen_added")
        rec_loaded = sems("rec_loaded", 2)
        gathered = sems("gathered", RING)
        sel_steps = sem("sel_steps")
        sel_ready = sem("sel_ready")
        passed = sem("passed")
        added = sem("added")
        blk_loaded = sem("blk_loaded")
        bc_ready = sem("bc_ready")
        b_done = sem("b_done")
        h_used = sem("h_used")
        b_ready = sem("b_ready")
        sn_ready = sem("sn_ready")
        blk_steps = sem("blk_steps")
        val_ready = sem("val_ready")
        diff_ready = sem("diff_ready")
        abs_ready = sem("abs_ready")
        out_done = sem("out_done")
        blk_done = sem("blk_done")
        bn_steps = sem("bn_steps")
        bn_var = sem("bn_var")
        bn_root = sem("bn_root")
        bn_ready = sem("bn_ready")
        fx_loaded = sems("fx_loaded", 2)
        y_ready = sems("y_ready", 2)
        y_turned = sems("y_turned", 2)
        fin_ready = sems("fin_ready", 2)
        out_stored = sems("out_stored", 2)

        def super_rows(t, s, n=SUPER, rows=P):
            if n == 1:
                return t[full * P:full * P + rows, :].rearrange("(c p) n -> p c n", c=1)
            return t[bass.ds(s * (SUPER * P), SUPER * P), :].rearrange("(c p) n -> p c n", c=SUPER)

        def all_supers(engine, work):
            if pairs > 1:
                with engine.Fori(0, pairs) as k:
                    for u in (0, 1):
                        work(k, u, SUPER, P)
            else:
                for u in (0, 1):
                    work(0, u, SUPER, P)
            work(pairs, 0, 1, tail_rows)

        def staggered(engine, first, second):
            first(0, 0, SUPER, P)
            if pairs > 1:
                with engine.Fori(0, pairs - 1) as k:
                    first(k, 1, SUPER, P)
                    second(k, 0, SUPER, P)
                    first(k + 1, 0, SUPER, P)
                    second(k, 1, SUPER, P)
            k = pairs - 1
            first(k, 1, SUPER, P)
            second(k, 0, SUPER, P)
            first(pairs, 0, 1, tail_rows)
            second(k, 1, SUPER, P)
            second(pairs, 0, 1, tail_rows)

        def before(u, k):
            return (0, k + 1) if u else (1, k)

        def edge_loop(engine, body, ends=None):
            with engine.Fori(0, LAG) as i:
                body(i, GROUPS, False)
            with engine.Fori(LAG, iters) as i:
                body(i, GROUPS, True)
            if rest:
                body(iters, rest, False)

        def block_nodes(j, w):
            return bass.ds(j * NB, w)

        last_blocks = [(j, NB if j < iters - 1 else last_nb) for j in range(iters - LAG, iters)]

        def carry_waits(engine):
            engine.sem_inc(waits_carried, 1)

        def fast(engine):
            engine.wait_ge(flag_ready, 1)
            return engine.value_load(flag[0:1, 0:1], min_val=0, max_val=1)

        block = ctx.enter_context(nc.Block())

        @block.sync
        def _(sp):
            sp.wait_ge(edges_cleared, 3)
            for a, to in ((src, raw_i[0]), (dst, raw_i[1])):
                if full_rb:
                    sp.dma_start(to[:, 0:full_rb, :],
                                 a[0:full_rb * P * P].rearrange("(r t e) -> t r e", r=full_rb, t=P)).then_inc(edges_loaded, 16)
                if rest_rows:
                    sp.dma_start(to[0:rest_rows, full_rb, :],
                                 a[full_rb * P * P:(full_rb * P + rest_rows) * P].rearrange("(t e) -> t e", e=P)
                                 ).then_inc(edges_loaded, 16)
                if tail_edges:
                    sp.dma_start(to[rest_rows:rest_rows + 1, full_rb, 0:tail_edges],
                                 a[(full_rb * P + rest_rows) * P:E].rearrange("(t e) -> t e", t=1)).then_inc(edges_loaded, 16)
            if full_rb:
                sp.dma_start(eig_sb[:, 0:full_rb, :],
                             eig[0:full_rb * P * P, :].rearrange("(r t e) k -> t r (e k)", r=full_rb, t=P)
                             ).then_inc(edges_loaded, 16)
            if rest_rows:
                sp.dma_start(eig_sb[0:rest_rows, full_rb, :],
                             eig[full_rb * P * P:(full_rb * P + rest_rows) * P, :].rearrange("(t e) k -> t (e k)", e=P)
                             ).then_inc(edges_loaded, 16)
            if tail_edges:
                sp.dma_start(eig_sb[rest_rows:rest_rows + 1, full_rb, 0:2 * tail_edges],
                             eig[(full_rb * P + rest_rows) * P:E, :].rearrange("(t e) k -> t (e k)", t=1)
                             ).then_inc(edges_loaded, 16)

            def load_x(k, u, n, rows):
                sp.wait_ge(xh_stored[u], 16 * k)
                sp.dma_start(x_sb[u][0:rows, 0:n, :], super_rows(x, 2 * k + u, n, rows)).then_inc(x_loaded[u], 16)

            for u in (0, 1):
                load_x(0, u, SUPER, P)
            sp.wait_ge(recs_ready, 1)
            sp.dma_start(rec_dram, recs).then_inc(recs_stored, 16)
            if pairs > 1:
                with sp.Fori(1, pairs) as k:
                    for u in (0, 1):
                        load_x(k, u, SUPER, P)
            load_x(pairs, 0, 1, tail_rows)
            sp.wait_ge(recs_stored, 16)

            with sp.If(fast(sp) == 0):
                with sp.Fori(0, rounds) as r:
                    with sp.Fori(0, slots) as t:
                        sp.wait_ge(gen_added, r * slots + t)
                        sp.dma_start(gen_rec, rec_dram[:, bass.ds(t, 1), :].rearrange("p t k -> p (t k)")).then_inc(gen_loaded, 16)
                sp.wait_ge(gen_added, rounds * slots)
            sp.nop()

            def load_block(j, w):
                sp.wait_ge(diff_ready, j)
                sp.wait_ge(h_used, j)
                sp.dma_start(h_blk[:, :, 0:w], h_t_dram[:, :, block_nodes(j, w)].rearrange("h p n -> p h n")).then_inc(blk_loaded, 16)
                sp.wait_ge(bc_ready, j)
                sp.dma_start(sn_row[:, 0:w], snorm[block_nodes(j, w), :].rearrange("n k -> k n")).then_inc(blk_loaded, 16)

            def body(i, n, with_block):
                for half in range(2):
                    if half * HALF < n:
                        m = min(HALF, n - half * HALF)
                        sp.wait_ge(passed, i * GROUPS + half * HALF + RING - HALF)
                        sp.dma_start(rec[:, half, 0:m * TILES, :],
                                     rec_dram[:, bass.ds(i * (GROUPS * TILES) + half * HALF * TILES, m * TILES), :]
                                     ).then_inc(rec_loaded[half], 16)
                    if half == 0 and with_block:
                        load_block(i - LAG, NB)

            edge_loop(sp, body)
            for j, w in last_blocks:
                load_block(j, w)

            sp.wait_ge(bc_ready, iters)

            def load_xh(k, u, n, rows):
                sp.wait_ge(out_stored[u], 16 * k)
                sp.dma_start(fin_x[u][0:rows, 0:n, :], super_rows(xh_dram, 2 * k + u, n, rows)).then_inc(fx_loaded[u], 16)

            all_supers(sp, load_xh)

        @block.gpsimd
        def _(pool):
            pool.memset(raw_i[0][:, full_rb, :], 0).then_inc(edges_cleared, 1)
            pool.memset(raw_i[1][:, full_rb, :], -1).then_inc(edges_cleared, 1)
            pool.memset(eig_sb[:, full_rb, :], 0.0).then_inc(edges_cleared, 1)
            pool.memset(ident[:, :], 0.0).then_inc(consts, 1)
            pool.memset(ones[:, :], 1.0).then_inc(consts, 1)
            pool.memset(eps[:, :], LN_EPS).then_inc(consts, 1)
            pool.iota(iota_i[:, 0:WINDOW], [[1, WINDOW]], base=0, channel_multiplier=0).then_inc(consts, 1)
            pool.iota(thr_i[:, 0:iters * GROUPS], [[NB, iters], [0, GROUPS]], base=(1 - LAG) * NB,
                      channel_multiplier=0).then_inc(thresholds, 1)
            if rest:
                pool.iota(thr_i[:, iters * GROUPS:groups], [[0, rest]], base=(iters + 1 - LAG) * NB,
                          channel_multiplier=0).then_inc(thresholds, 1)
            pool.wait_ge(consts, 4)
            pool.affine_select(out=ident[:, :], in_=ident[:, :], compare_op=ALU.not_equal, fill=1.0, base=0,
                               pattern=[[-1, P]], channel_multiplier=1).then_inc(consts, 1)
            for v in range(SUMS):
                for h in range(HALVES):
                    if v * HALVES + h < 3:
                        pool.memset(table[:, v, h, :], 0.0).then_inc(zeroed, 1)

            pool.wait_ge(recs_stored, 16)
            pool.memset(table[:, 2, 1, :], 0.0).then_inc(zeroed2, 1)

            def residual(k, u, n, rows):
                pool.wait_ge(h_ready[u], SUPER * k + n)
                pool.tensor_tensor(x_sb[u][0:rows, 0:n, :], x_sb[u][0:rows, 0:n, :], h_sb[u][0:rows, 0:n, :],
                                   ALU.add).then_inc(xh_ready[u], 1)
                pool.wait_ge(xh_ready[u], k + 1)
                pool.dma_start(super_rows(xh_dram, 2 * k + u, n, rows), x_sb[u][0:rows, 0:n, :]).then_inc(xh_stored[u], 16)
                for p in range(2 if n > 1 else 1):
                    pool.wait_ge(ht_copied[u][p], k + 1)
                to = h_t_dram[:, :, bass.ds((2 * k + u) * (SUPER * P), n * P)].rearrange("h p n -> p h n")
                if n == 1:
                    to = h_t_dram[:, :, full * P:full * P + rows].rearrange("h p n -> p h n")
                pool.dma_start(to, ht_sb[u][:, :, 0:(n * P if n > 1 else rows)]).then_inc(ht_stored[u], 16)

            all_supers(pool, residual)
            pool.wait_ge(a_stored[0], 16 * (pairs + 1))
            pool.wait_ge(a_stored[1], 16 * pairs)
            with pool.If(fast(pool) == 0):
                with pool.Fori(0, rounds) as r:
                    with pool.Fori(0, slots) as t:
                        pool.wait_ge(gen_loaded, 16 * (r * slots + t + 1))
                        pool.wait_ge(gen_added, r * slots + t)
                        carry_waits(pool)
                        pool.indirect_dma_start(
                            out=gen_rows, out_offset=None, in_=a_dram,
                            in_offset=bass.IndirectOffsetOnAxis(ap=gen_rec[:, SRC:SRC + 1].bitcast(U32), axis=0),
                        ).then_inc(gen_gathered, 16)
                pool.wait_ge(gen_added, rounds * slots)
            pool.nop()

            def body(i, n, with_block):
                for q in range(n):
                    if q % HALF == 0:
                        pool.wait_ge(rec_loaded[q // HALF], 16 * (i + 1))
                    pool.wait_ge(passed, i * GROUPS + q + 1)
                    carry_waits(pool)
                    for t in range(TILES):
                        pool.indirect_dma_start(
                            out=ring[:, (q % RING) * TILES + t, :], out_offset=None, in_=a_dram,
                            in_offset=bass.IndirectOffsetOnAxis(
                                ap=rec[:, q // HALF, (q % HALF) * TILES + t, SRC:SRC + 1].bitcast(U32), axis=0),
                        ).then_inc(gathered[q % RING], 16)

            edge_loop(pool, body)

        @block.tensor
        def _(pe):
            pe.wait_ge(consts, 5)
            fill = 0
            for a in range(3):
                pe.wait_ge(edges_float, a + 1)
                for first in range(0, rows_in, 4):
                    if fill >= 4:
                        pe.wait_ge(edges_copied, fill - 3)
                    for r in range(first, min(first + 4, rows_in)):
                        rows = min(P, slots - r * P)
                        last = pe.transpose(bank[fill % 4][:, (r - first) * P:(r - first) * P + rows],
                                            raw_f[a][0:rows, r, :], ident[0:rows, 0:rows])
                    last.then_inc(edges_turned, 1)
                    fill += 1
            pe.wait_ge(edges_copied, fill)
            pe.matmul(bank[0][:, 0:groups], ones[0:1, :], recs[0:1, 0:slots:TILES, DST], start=True, stop=True
                      ).then_inc(base_spread, 1)
            pe.wait_ge(voted, 1)
            pe.matmul(bank[1][:, 0:1], ones[:, :], vote, start=True, stop=True).then_inc(vote_sum, 1)

            def turn(k, u, n, rows):
                for p in range(2 if n > 1 else 1):
                    pe.wait_ge(h_ready[u], SUPER * k + min(2 * p + 2, n))
                    b, done = before(u, k)
                    pe.wait_ge(ht_copied[b][p], done)
                    for c in range(min(2, n)):
                        for h in range(HALVES):
                            last = pe.transpose(t_ps[p][:, c, h, 0:rows], h_sb[u][0:rows, 2 * p + c, h * P:(h + 1) * P],
                                                ident[0:rows, 0:rows])
                    last.then_inc(h_turned[u][p], 1)

            def product(k, u, n, rows):
                for p in range(2 if n > 1 else 1):
                    pe.wait_ge(ht_copied[u][p], k + 1)
                    b, done = before(u, k)
                    pe.wait_ge(a_copied[b][p], done)
                    for c in range(min(2, n)):
                        m = (2 * p + c) * P
                        for h in range(HALVES):
                            last = pe.matmul(a_ps[p][0:rows, c, :], ht_sb[u][:, h, m:m + rows], w1a[:, h, :],
                                             start=(h == 0), stop=(h == HALVES - 1))
                    last.then_inc(a_done[u][p], 1)

            pe.wait_ge(w_loaded, 48)
            staggered(pe, turn, product)

            with pe.If(fast(pe) == 0):
                with pe.Fori(0, rounds) as r:
                    with pe.Fori(0, slots) as t:
                        pe.wait_ge(gen_sel_ready, r * slots + t + 1)
                        pe.wait_ge(gen_gathered, 16 * (r * slots + t + 1))
                        for h in range(HALVES):
                            pe.matmul(bank[h][:, 0:SUMS * P], gen_rows[:, h * P:(h + 1) * P],
                                      gen_sel[:, :, :].rearrange("p v n -> p (v n)"), start=True, stop=True)
                        pe.matmul(bank[2][0:SUMS, 0:P], gen_rec[:, ONE:ONE + SUMS], gen_sel[:, 0, :],
                                  start=True, stop=True).then_inc(gen_summed, 1)
                pe.wait_ge(gen_added, rounds * slots)
            pe.nop()
            pe.sem_inc(passed, RING)

            def sum_group(i, q):
                g = i * GROUPS + q
                ps = group_ps[q % 2]
                pe.wait_ge(added, g)
                pe.wait_ge(sel_ready, g + 1)
                pe.wait_ge(gathered[q % RING], 16 * TILES * ((GROUPS // RING) * i + q // RING + 1))
                for t in range(TILES):
                    for h in range(HALVES):
                        pe.matmul(ps[:, h * SEL:(h + 1) * SEL], ring[:, (q % RING) * TILES + t, h * P:(h + 1) * P],
                                  sel[:, q % 2, t, :, :].rearrange("p v n -> p (v n)"),
                                  start=(t == 0 and h == 0), stop=(t == TILES - 1), skip_group_check=True)
                    last = pe.matmul(ps[0:SUMS, HALVES * SEL:HALVES * SEL + WINDOW],
                                     rec[:, q // HALF, (q % HALF) * TILES + t, ONE:ONE + SUMS],
                                     sel[:, q % 2, t, 0, :], start=False, stop=(t == TILES - 1), skip_group_check=True)
                last.then_inc(passed, 1)

            def spread_sums(j, w, groups_done):
                pe.wait_ge(added, groups_done + 1)
                pe.wait_ge(blk_loaded, 32 * j + 32)
                pe.wait_ge(blk_done, j)
                for v, to in enumerate((deg_bc, abs_bc, w_bc)):
                    pe.matmul(to[:, 0:w], pick[0:SUMS, v, :], sums[0:SUMS, block_nodes(j, w)], start=True, stop=True,
                              skip_group_check=True)
                pe.matmul(sn_bc[:, 0:w], ones[0:1, :], sn_row[:, 0:w], start=True, stop=True,
                          skip_group_check=True).then_inc(bc_ready, 1)

            def b_block(j, w):
                for ho in range(HALVES):
                    for h in range(HALVES):
                        last = pe.matmul(b_ps[:, ho, 0:w], w1b[:, h, ho * P:(ho + 1) * P], h_blk[:, h, 0:w],
                                         start=(h == 0), stop=(h == HALVES - 1), skip_group_check=True)
                last.then_inc(b_done, 1)

            def out_part(c, w, rhs):
                for h in range(HALVES):
                    for ho in range(HALVES):
                        last = pe.matmul(out_ps[:, ho, 0:w], w2[:, c * HALVES + h, ho * P:(ho + 1) * P], rhs[:, h, 0:w],
                                         start=(c == 0 and h == 0 and ho == 0), stop=(c == SUMS and h == HALVES - 1),
                                         skip_group_check=True)
                return last

            def block_part(q, j, w, groups_done):
                if q == 0:
                    spread_sums(j, w, groups_done)
                if q == 1:
                    b_block(j, w)
                    out_part(0, w, h_blk).then_inc(h_used, 1)
                if q in (3, 4):
                    pe.wait_ge(val_ready, 2 * j + q - 2)
                    out_part(q - 2, w, val[:, q - 3])
                if q == 5:
                    pe.wait_ge(abs_ready, j + 1)
                    out_part(SUMS, w, val[:, SUMS - 1]).then_inc(out_done, 1)

            def body(i, n, with_block):
                for q in range(n):
                    sum_group(i, q)
                    if with_block:
                        block_part(q, i - LAG, NB, i * GROUPS)

            edge_loop(pe, body)
            for j, w in last_blocks:
                for q in range(GROUPS):
                    block_part(q, j, w, groups)

            def turn_back(k, u, n, rows):
                pe.wait_ge(y_ready[u], k + 1)
                pe.wait_ge(fin_ready[u], k)
                for c in range(n):
                    for h in range(HALVES):
                        m = c * P if n > 1 else 0
                        last = pe.transpose(bank[2 * u + c // 2][0:rows, (c % 2) * D + h * P:(c % 2) * D + (h + 1) * P],
                                            fin_y[u][:, h, m:m + rows], ident[:, :])
                last.then_inc(y_turned[u], 1)

            all_supers(pe, turn_back)

        @block.scalar
        def _(act):
            for w, to in ((W1[0:D, :], w1a), (W1[D:2 * D, :], w1b[:, :, :]), (W2, w2[:, :, :])):
                act.dma_start(to, w.rearrange("(k p) n -> p k n", p=P)).then_inc(w_loaded, 16)
            for v, to in ((b1, b1_t), (b2, b2_t), (gamma, gamma_t), (beta, beta_t)):
                act.dma_start(to[:, :], v.rearrange("(h p) -> p h", p=P)).then_inc(small_loaded, 16)

            def normal(k, u, n, rows):
                act.wait_ge(var_ready, 2 * k + u + 1)
                act.activation(std[u][0:rows, 0:n], mv[u][0:rows, 0:n, 1], ACT.Sqrt, bias=eps[0:rows, :]).then_inc(std_ready, 1)
                act.wait_ge(scale_ready, 2 * k + u + 1)
                act.wait_ge(h_turned[u][1], k)
                act.wait_ge(xh_ready[u], k)
                for c in range(n):
                    act.activation(h_sb[u][0:rows, c, :], x_sb[u][0:rows, c, :], ACT.Relu, bias=shift[u][0:rows, c:c + 1],
                                   scale=rstd[u][0:rows, c:c + 1]).then_inc(h_ready[u], 1)

            def keep_a(k, u, n, rows):
                act.wait_ge(a_stored[u], 16 * k)
                for p in range(2 if n > 1 else 1):
                    act.wait_ge(a_done[u][p], k + 1)
                    m = min(2, n)
                    act.activation(a_sb[u][0:rows, 2 * p:2 * p + m, :], a_ps[p][0:rows, 0:m, :], ACT.Copy
                                   ).then_inc(a_copied[u][p], 1)
                for p in range(2 if n > 1 else 1):
                    act.wait_ge(a_copied[u][p], k + 1)
                act.dma_start(super_rows(a_dram, 2 * k + u, n, rows), a_sb[u][0:rows, 0:n, :]).then_inc(a_stored[u], 16)

            act.wait_ge(consts, 5)
            staggered(act, normal, keep_a)
            act.wait_ge(small_loaded, 64)

            def block_part(q, j, w):
                if q == 0:
                    act.wait_ge(bc_ready, j + 1)
                    act.activation(sn[:, 0:w], sn_bc[:, 0:w], ACT.Copy).then_inc(sn_ready, 1)
                if q == 1:
                    act.wait_ge(b_done, j + 1)
                    for h in range(HALVES):
                        last = act.activation(b_rows[:, h, 0:w], b_ps[:, h, 0:w], ACT.Identity, bias=b1_t[:, h:h + 1])
                    last.then_inc(b_ready, 1)
                if q == 4:
                    act.wait_ge(diff_ready, j + 1)
                    act.activation(val[:, SUMS - 1, :, 0:w], val[:, SUMS - 1, :, 0:w], ACT.Abs).then_inc(abs_ready, 1)

            with act.Fori(0, iters - LAG) as j:
                for q in range(GROUPS):
                    block_part(q, j, NB)
            for j, w in last_blocks:
                for q in range(GROUPS):
                    block_part(q, j, w)

            act.wait_ge(bn_var, 1)
            act.activation(bn_std, bn_mv[:, :, 1], ACT.Sqrt, bias=eps[:, :]).then_inc(bn_root, 1)
            act.wait_ge(bn_ready, 1)

            def activate(k, u, n, rows):
                act.wait_ge(y_turned[u], k)
                w = n * P if n > 1 else rows
                m = bass.ds((2 * k + u) * (SUPER * P), w) if n > 1 else bass.ds(full * P, w)
                for h in range(HALVES):
                    last = act.activation(fin_y[u][:, h, 0:w], table[:, 0, h, m], ACT.Relu, bias=bn_shift[:, h:h + 1],
                                          scale=bn_scale[:, h:h + 1])
                last.then_inc(y_ready[u], 1)

            def store(k, u, n, rows):
                act.wait_ge(fin_ready[u], k + 1)
                act.dma_start(super_rows(out, 2 * k + u, n, rows), fin_x[u][0:rows, 0:n, :]).then_inc(out_stored[u], 16)

            staggered(act, activate, store)
            act.wait_ge(out_stored[0], 16 * (pairs + 1))
            act.wait_ge(out_stored[1], 16 * pairs)

        @block.vector
        def _(dve):
            chained = [0]

            def link(ins):
                chained[0] += 1
                ins.then_inc(prep, 1)
                dve.wait_ge(prep, chained[0])

            per_array = bool(full_rb) + bool(rest_rows) + bool(tail_edges)
            dve.wait_ge(edges_loaded, 48 * per_array)
            for a in range(2):
                dve.tensor_copy(raw_f[a], raw_i[a]).then_inc(edges_float, 1)
            dve.tensor_copy(raw_f[2], eig_sb[:, :, :].rearrange("p r (e k) -> p r e k", k=2)[:, :, :, 0]).then_inc(edges_float, 1)
            dve.wait_ge(consts, 5)
            dve.tensor_copy(nodes_iota[:, :], iota_i[:, 0:WINDOW])
            for v in range(SUMS):
                dve.tensor_copy(pick[0:SUMS, v, :], ident[0:SUMS, v:v + 1].to_broadcast([SUMS, P]))
            dve.memset(bases[:, :, :], 0)
            dve.memset(recs[:, :, ONE], 1.0).then_inc(picked, 1)
            fill = 0
            for a, word in enumerate((SRC, DST, ONE + 2)):
                for first in range(0, rows_in, 4):
                    m = min(4 * P, slots - first * P)
                    dve.wait_ge(edges_turned, fill + 1)
                    to = recs[:, first * P:first * P + m, word]
                    dve.tensor_copy(to.bitcast(I32) if word == SRC else to, bank[fill % 4][:, 0:m]).then_inc(edges_copied, 1)
                    fill += 1
            dve.wait_ge(edges_copied, fill)
            dve.scalar_tensor_tensor(out=recs[:, :, ONE + 1], in0=recs[:, :, ONE + 2], scalar=-1.0,
                                     in1=recs[:, :, ONE + 2], op0=ALU.mult, op1=ALU.max)
            dve.wait_ge(picked, 1)
            base_f = recs[0:1, 0:slots:TILES, DST]
            dve.tensor_copy(bases[:, 0:iters, 0:GROUPS], base_f[:, 0:iters * GROUPS].rearrange("p (i q) -> p i q", q=GROUPS))
            if rest:
                dve.tensor_copy(bases[:, iters, 0:rest], base_f[:, iters * GROUPS:groups])
            dve.wait_ge(base_spread, 1)
            rel = recs[:, :, REL]
            link(dve.tensor_tensor(recs[:, :, REL].rearrange("p (g t) -> p g t", t=TILES),
                                   recs[:, :, DST].rearrange("p (g t) -> p g t", t=TILES),
                                   bank[0][:, 0:groups].unsqueeze(2).to_broadcast([P, groups, TILES]), ALU.subtract))
            link(dve.tensor_single_scalar(mask[0], rel, 0.0, ALU.is_ge))
            link(dve.scalar_tensor_tensor(out=mask[1], in0=rel, scalar=float(WINDOW - 1), in1=mask[0],
                                          op0=ALU.is_le, op1=ALU.mult))
            link(dve.tensor_reduce(count[:, 0:1], mask[1], AX_X, ALU.add))
            dve.wait_ge(thresholds, 2 if rest else 1)
            link(dve.tensor_copy(mask[0][:, 0:groups], thr_i[:, 0:groups]))
            link(dve.tensor_tensor(mask[2][:, 0:groups], mask[0][:, 0:groups], bank[0][:, 0:groups], ALU.is_le))
            link(dve.tensor_reduce(count[:, 1:2], mask[2][:, 0:groups], AX_X, ALU.add))
            dve.tensor_tensor(vote, count[:, 0:1], count[:, 1:2], ALU.add).then_inc(voted, 1)

            dve.wait_ge(vote_sum, 1)
            link(dve.tensor_single_scalar(ok, bank[1][:, 0:1], float(E + P * groups), ALU.is_equal))
            dve.tensor_copy(flag[:, :], ok).then_inc(flag_ready, 1)
            link(dve.tensor_single_scalar(ok_less_1, ok, -1.0, ALU.add))
            dve.tensor_scalar(rel, rel, ok, ok_less_1, ALU.mult, ALU.add).then_inc(recs_ready, 1)
            for v, h in ((1, 1), (2, 0)):
                dve.memset(table[:, v, h, :], 0.0)
            dve.wait_ge(recs_ready, 1)

            def statistics(k, u, n, rows):
                s = 2 * k + u
                dve.wait_ge(x_loaded[u], 16 * (k + 1))
                for c in range(n):
                    last = dve.bn_stats(stats6[0:rows, c, :], x_sb[u][0:rows, c, :])
                last.then_inc(ln_steps, 1)
                dve.wait_ge(ln_steps, 2 * s + 1)
                carry_waits(dve)
                for c in range(n):
                    last = dve.bn_aggr(mv[u][0:rows, c, :], stats6[0:rows, c, :])
                last.then_inc(var_ready, 1)
                dve.wait_ge(std_ready, s + 1)
                dve.reciprocal(rstd[u][0:rows, 0:n], std[u][0:rows, 0:n]).then_inc(ln_steps, 1)
                dve.wait_ge(ln_steps, 2 * s + 2)
                dve.wait_ge(var_ready, s + 1)
                dve.scalar_tensor_tensor(out=shift[u][0:rows, 0:n], in0=mv[u][0:rows, 0:n, 0], scalar=-1.0,
                                         in1=rstd[u][0:rows, 0:n], op0=ALU.mult, op1=ALU.mult).then_inc(scale_ready, 1)

            def keep_ht(k, u, n, rows):
                dve.wait_ge(ht_stored[u], 16 * k)
                for p in range(2 if n > 1 else 1):
                    dve.wait_ge(h_turned[u][p], k + 1)
                    if n > 1:
                        to = ht_sb[u][:, :, 2 * p * P:(2 * p + 2) * P].rearrange("p h (c n) -> p c h n", c=2)
                        dve.tensor_copy(to, t_ps[p]).then_inc(ht_copied[u][p], 1)
                    else:
                        dve.tensor_copy(ht_sb[u][:, :, 0:rows], t_ps[p][:, 0, :, 0:rows]).then_inc(ht_copied[u][p], 1)

            staggered(dve, statistics, keep_ht)

            for u in (0, 1):
                dve.wait_ge(xh_stored[u], 16 * (pairs + 1 - u))
                dve.wait_ge(ht_stored[u], 16 * (pairs + 1 - u))
                dve.wait_ge(a_done[u][0], pairs + 1 - u)
                dve.wait_ge(a_done[u][1], pairs)
            dve.memset(sums[0:SUMS, :], 0.0).then_inc(sums_zeroed, 1)
            dve.wait_ge(sums_zeroed, 1)
            dve.wait_ge(zeroed, 3)
            dve.wait_ge(recs_stored, 16)
            dve.wait_ge(zeroed2, 1)

            with dve.If(fast(dve) == 0):
                for m in range(P // WINDOW):
                    last = dve.tensor_single_scalar(gen_nodes[:, m * WINDOW:(m + 1) * WINDOW], nodes_iota[:, :],
                                                    float(m * WINDOW), ALU.add)
                last.then_inc(gen_steps, 1)
                with dve.Fori(0, rounds) as r:
                    with dve.Fori(0, slots) as t:
                        n = r * slots + t
                        dve.wait_ge(gen_steps, n + r + 1)
                        dve.wait_ge(gen_loaded, 16 * (n + 1))
                        dve.tensor_scalar(gen_sel[:, 0, :], gen_nodes, gen_rec[:, DST:DST + 1], None, ALU.is_equal
                                          ).then_inc(gen_steps, 1)
                        dve.wait_ge(gen_steps, n + r + 2)
                        dve.tensor_scalar(gen_sel[:, 2, :], gen_sel[:, 0, :], gen_rec[:, ONE + 2:ONE + 3], None, ALU.mult)
                        dve.tensor_scalar(gen_sel[:, 1, :], gen_sel[:, 0, :], gen_rec[:, ONE + 1:ONE + 2], None, ALU.mult
                                          ).then_inc(gen_sel_ready, 1)
                        dve.wait_ge(gen_summed, n + 1)
                        nodes = bass.ds(r * P, P)
                        for h in range(HALVES):
                            dve.tensor_tensor(table[:, :, h, nodes], table[:, :, h, nodes],
                                              bank[h][:, 0:SUMS * P].rearrange("p (v n) -> p v n", v=SUMS), ALU.add)
                        dve.tensor_tensor(sums[0:SUMS, nodes], sums[0:SUMS, nodes], bank[2][0:SUMS, 0:P], ALU.add
                                          ).then_inc(gen_added, 1)
                        dve.wait_ge(gen_added, n + 1)
                    dve.tensor_single_scalar(gen_nodes, gen_nodes, float(P), ALU.add).then_inc(gen_steps, 1)
            dve.nop()
            dve.sem_inc(added, 1)
            base_regs = [dve.alloc_register(f"base{q}") for q in range(GROUPS)]

            def select(i, q):
                g = i * GROUPS + q
                if q % HALF == 0:
                    dve.wait_ge(rec_loaded[q // HALF], 16 * (i + 1))
                dve.wait_ge(passed, g + RING - 1)
                r = rec[:, q // HALF, (q % HALF) * TILES:(q % HALF + 1) * TILES, :]
                s = sel[:, q % 2]
                dve.tensor_tensor(s[:, :, 0, :], nodes_iota[:, :].unsqueeze(1).to_broadcast([P, TILES, WINDOW]),
                                  r[:, :, REL:REL + 1].to_broadcast([P, TILES, WINDOW]), ALU.is_equal).then_inc(sel_steps, 1)
                dve.wait_ge(sel_steps, g + 1)
                dve.tensor_tensor(s[:, :, 1:SUMS, :], s[:, :, 0:1, :].to_broadcast([P, TILES, 2, WINDOW]),
                                  r[:, :, ONE + 1:ONE + 3].unsqueeze(3).to_broadcast([P, TILES, 2, WINDOW]),
                                  ALU.mult).then_inc(sel_ready, 1)

            def add(i, q, base):
                g = i * GROUPS + q
                ps = group_ps[q % 2]
                nodes = bass.ds(base, WINDOW)
                dve.wait_ge(passed, g + RING + 1)
                dve.wait_ge(added, g + 1)
                dve.tensor_tensor(table[:, :, :, nodes], table[:, :, :, nodes],
                                  ps[:, 0:HALVES * SEL].rearrange("p (h v n) -> p v h n", h=HALVES, v=SUMS), ALU.add)
                dve.tensor_tensor(sums[0:SUMS, nodes], sums[0:SUMS, nodes],
                                  ps[0:SUMS, HALVES * SEL:HALVES * SEL + WINDOW], ALU.add).then_inc(added, 1)

            STEPS = 10

            def block_part(q, j, w):
                nodes = block_nodes(j, w)

                def step(n, ins):
                    ins.then_inc(blk_steps, 1)
                    dve.wait_ge(blk_steps, j * STEPS + n)

                def value(v, spread, inverse, n):
                    to = val[:, v, :, 0:w]
                    step(n, dve.tensor_tensor(to, b_rows[:, :, 0:w], spread[:, 0:w].unsqueeze(1).to_broadcast([P, HALVES, w]), ALU.mult))
                    step(n + 1, dve.tensor_tensor(to, to, table[:, v, :, nodes], ALU.add))
                    return dve.tensor_tensor(to, to, inverse[:, 0:w].unsqueeze(1).to_broadcast([P, HALVES, w]), ALU.mult)

                if q == 1:
                    dve.wait_ge(bc_ready, j + 1)
                    dve.tensor_single_scalar(inv_deg[:, 0:w], deg_bc[:, 0:w], 1.0, ALU.max)
                    step(1, dve.tensor_single_scalar(inv_abs[:, 0:w], abs_bc[:, 0:w], SUM_EPS, ALU.add))
                    dve.reciprocal(inv_deg[:, 0:w], inv_deg[:, 0:w])
                    step(2, dve.reciprocal(inv_abs[:, 0:w], inv_abs[:, 0:w]))
                if q == 2:
                    dve.wait_ge(b_ready, j + 1)
                    value(0, deg_bc, inv_deg, 3).then_inc(val_ready, 1)
                if q == 3:
                    value(1, abs_bc, inv_abs, 5).then_inc(val_ready, 1)
                if q == 4:
                    step(9, value(2, w_bc, inv_abs, 7))
                    dve.tensor_tensor(val[:, 2, :, 0:w], val[:, 2, :, 0:w], h_blk[:, :, 0:w], ALU.subtract).then_inc(diff_ready, 1)
                if q == 6:
                    dve.wait_ge(out_done, j + 1)
                    dve.wait_ge(sn_ready, j + 1)
                    for h in range(HALVES):
                        last = dve.scalar_tensor_tensor(out=table[:, 0, h, nodes], in0=out_ps[:, h, 0:w],
                                                        scalar=b2_t[:, h:h + 1], in1=sn[:, 0:w], op0=ALU.add, op1=ALU.mult)
                    step(10, last)
                    for h in range(HALVES):
                        last = dve.bn_stats(bn[:, h, bass.ds(j, 1), :].rearrange("p a k -> p (a k)"), table[:, 0, h, nodes])
                    last.then_inc(blk_done, 1)

            def body(i, n, with_block):
                dve.reg_load(base_regs[0:n], bases[0:1, bass.ds(i, 1), 0:n].rearrange("p a k -> p (a k)"))
                base = [dve.snap(r, min_val=0, max_val=N - 1) for r in base_regs[0:n]]
                for q in range(n):
                    select(i, q)
                    if q:
                        add(i, q - 1, base[q - 1])
                    if with_block:
                        block_part(q, i - LAG, NB)
                add(i, n - 1, base[n - 1])
                if with_block:
                    block_part(GROUPS, i - LAG, NB)

            dve.wait_ge(small_loaded, 64)
            edge_loop(dve, body)
            for j, w in last_blocks:
                for q in range(GROUPS + 1):
                    block_part(q, j, w)

            chain = [0]

            def bn_link(ins):
                chain[0] += 1
                ins.then_inc(bn_steps, 1)
                dve.wait_ge(bn_steps, chain[0])

            dve.wait_ge(blk_done, iters)
            for h in range(HALVES):
                last = dve.bn_aggr(bn_mv[:, h, :], bn[:, h, :, :].rearrange("p a k -> p (a k)"))
            last.then_inc(bn_var, 1)
            dve.wait_ge(bn_root, 1)
            bn_link(dve.reciprocal(bn_std, bn_std))
            bn_link(dve.tensor_tensor(bn_scale, bn_std, gamma_t[:, :], ALU.mult))
            bn_link(dve.tensor_tensor(bn_shift, bn_mv[:, :, 0], bn_scale, ALU.mult))
            dve.tensor_tensor(bn_shift, beta_t[:, :], bn_shift, ALU.subtract).then_inc(bn_ready, 1)

            def finish(k, u, n, rows):
                dve.wait_ge(fx_loaded[u], 16 * (k + 1))
                dve.wait_ge(y_turned[u], k + 1)
                for c in range(0, n, 2):
                    m = min(2, n)
                    to = fin_x[u][0:rows, c:c + m, :]
                    last = dve.tensor_tensor(to, to, bank[2 * u + c // 2][0:rows, 0:m * D].rearrange("p (c n) -> p c n", c=m), ALU.add)
                last.then_inc(fin_ready[u], 1)

            all_supers(dve, finish)


_INS = ["x", "src", "dst", "edge_attr_2", "node_vec1", "L0_gnn_W1", "L0_gnn_b1", "L0_gnn_W2", "L0_gnn_b2",
        "L0_gnn_gamma", "L0_gnn_beta"]


def kernel(**inputs):
    import numpy as np
    import concourse.bacc as bacc
    from concourse.bass_utils import run_bass_kernel_spmd

    nc = bacc.Bacc("TRN2", target_bir_lowering=False, num_devices=1)
    arrays, args = {}, []
    for name in _INS:
        a = np.ascontiguousarray(inputs[name])
        arrays[f"in_{name}"] = a
        args.append(nc.dram_tensor(f"in_{name}", a.shape, mybir.dt.from_np(a.dtype), kind="ExternalInput").ap())
    out = nc.dram_tensor("out", inputs["x"].shape, F32, kind="ExternalOutput").ap()
    with nc.allow_non_contiguous_dma("four vectors of 256 features, one feature a partition"):
        build(nc, *args, out)
    r = run_bass_kernel_spmd(nc, [arrays], core_ids=[0])
    return r.results[0]["out"]
```

```python
from contextlib import ExitStack

import concourse.bass as bass
from concourse import mybir

F32 = mybir.dt.float32
I32 = mybir.dt.int32
U32 = mybir.dt.uint32
ALU = mybir.AluOpType
ACT = mybir.ActivationFunctionType
AX_X = mybir.AxisListType.X

P = 128
D = 256
HALVES = D // P
SUMS = 3
TILES = 3
WINDOW = 32
GROUPS = 4
RING = GROUPS
UNIT = GROUPS * TILES
WORDS = 6
SRC, DST, REL, ONE = 0, 1, 2, 3
SUPER = 4
SEL = SUMS * WINDOW
LN_EPS = 1e-5
BN_EPS = 1e-5
SUM_EPS = 1e-8


def build(nc, x, src, dst, eig, snorm, W1, b1, W2, b2, gamma, beta, out):
    N = x.shape[0]
    E = src.shape[0]
    tiles = -(-E // P)
    groups = -(-tiles // TILES)
    slots = groups * TILES
    units, rest = divmod(groups, GROUPS)
    margin = -(-N // units)
    NB = 2 * margin
    unit_pairs = units // 2
    last_nb = N - (unit_pairs * NB - margin)
    full, tail_rows = divmod(N, P)
    supers = full // SUPER
    pairs = supers // 2
    rounds = -(-N // P)
    EARLY = 2048
    NP = -(-max(N + WINDOW, rounds * P, 6 * SUPER * D) // 16) * 16
    rows_in = -(-slots // P)
    full_rb, rest_rows = divmod(E // P, P)
    tail_edges = E % P
    assert full % (2 * SUPER) == 0 and pairs >= 1 and 0 < tail_rows and unit_pairs > 3 and 0 < last_nb <= NB
    assert rows_in == full_rb + 1 and groups <= 512 and HALVES * NB <= 512 and slots * WORDS <= NP

    h_t_dram = nc.dram_tensor("h_t", [HALVES, P, (full + 1) * P], F32).ap()
    a_dram = nc.dram_tensor("a_rows", [N, D], F32).ap()
    xh_dram = nc.dram_tensor("x_plus_h", [N, D], F32).ap()
    rec_dram = nc.dram_tensor("edge_records", [P, slots, WORDS], F32).ap()

    ctx = ExitStack()
    with ctx:
        def sb(name, shape, dt=F32):
            return ctx.enter_context(nc.sbuf_tensor(name, shape, dt))

        def sem(name):
            return ctx.enter_context(nc.semaphore(name))

        def sems(name, n):
            return [sem(f"{name}{k}") for k in range(n)]

        table = sb("table", [P, SUMS, HALVES, NP])
        sums = sb("sums", [P, NP])
        ring = sb("ring", [P, RING * TILES, D])
        w1b = sb("w1b", [P, HALVES, D])
        w2 = sb("w2", [P, 4 * HALVES, D])
        ident = sb("ident", [P, P])
        ones = sb("ones", [P, P])
        nodes_iota = sb("nodes_iota", [P, WINDOW])
        eps = sb("eps", [P, 1])
        b1_t = sb("b1_t", [P, HALVES])
        b2_t = sb("b2_t", [P, HALVES])
        gamma_t = sb("gamma_t", [P, HALVES])
        beta_t = sb("beta_t", [P, HALVES])
        rec = sb("rec", [P, 2, UNIT, WORDS])
        sel = sb("sel", [P, 2, TILES, SUMS, WINDOW])
        b_rows = sb("b_rows", [P, HALVES, NB])
        h_blk = sb("h_blk", [P, HALVES, NB])
        spread_b = sb("spread_b", [P, HALVES, NB])
        inv_rows = sb("inv_rows", [2, NB])
        abs_eps = sb("abs_eps", [2, 1])
        sn = sb("sn", [P, NB])
        bn = sb("bn", [P, HALVES, unit_pairs + 1, 6])
        bases = sb("bases", [1, units + 1, GROUPS], I32)
        ln_scale = sb("ln_scale", [P, full + 1])
        ln_shift = sb("ln_shift", [P, full + 1])
        small = sb("small", [P, 64])
        flag = sb("flag", [P, 1], I32)

        lnb = sums[:, 0:6 * SUPER * D].rearrange("p (k c n) -> p k c n", k=6, c=SUPER)
        x_sb = [lnb[:, k] for k in (0, 1)]
        h_sb = [lnb[:, k] for k in (2, 3)]
        ht_sb = [lnb[:, k].rearrange("p c n -> p (c n)").rearrange("p (h n) -> p h n", h=HALVES) for k in (4, 5)]
        a_sb = [ring[:, SUPER * k:SUPER * k + SUPER, :] for k in (0, 1)]
        w1a = sel[:, :, :, :, :].rearrange("p a t v n -> p (a t v n)")[:, 0:HALVES * D].rearrange("p (h n) -> p h n", h=HALVES)
        plane = [table[:, v, h, :] for v in range(SUMS) for h in range(HALVES)]
        raw = plane[3]
        raw_n = rows_in * P
        raw_i = [raw[:, k * raw_n:(k + 1) * raw_n].bitcast(I32).rearrange("p (r e) -> p r e", r=rows_in) for k in (0, 1)]
        raw_f = [raw[:, k * raw_n:(k + 1) * raw_n].rearrange("p (r e) -> p r e", r=rows_in) for k in (2, 3, 4)]
        mask = [plane[4][:, k * slots:(k + 1) * slots] for k in range(3)]
        eig_sb = plane[4][:, 3 * slots:3 * slots + 2 * raw_n].rearrange("p (r e) -> p r e", r=rows_in)
        thr_i = plane[4][:, 3 * slots + 2 * raw_n:3 * slots + 2 * raw_n + groups].bitcast(I32)
        iota_i = plane[4][:, 3 * slots + 2 * raw_n + groups:3 * slots + 2 * raw_n + groups + WINDOW].bitcast(I32)
        assert 3 * slots + 2 * raw_n + groups + WINDOW <= NP and 5 * raw_n <= NP
        recs = plane[5][:, 0:slots * WORDS].rearrange("p (t k) -> p t k", k=WORDS)
        STRIDE = NP // 4
        spare = table[:, 1:SUMS, :, :].rearrange("p v h n -> p (v h n)")
        scratch = plane[5][:, D:D + 4 * SUPER * D].rearrange("p (k m) -> p k m", k=4)
        fin_h = [scratch[:, k].rearrange("p (c n) -> p c n", c=SUPER) for k in (0, 1)]
        fin_y = [scratch[:, k].rearrange("p (h n) -> p h n", h=HALVES) for k in (2, 3)]
        done_early = (unit_pairs - 1) * NB - margin
        x_early = done_early >= max(3 * STRIDE + SUPER * D, 5 * SUPER * D)
        assert STRIDE >= SUPER * D and supers == 12 or supers < 12

        def fin_x(k, u, n, rows):
            first = (2 * k + u) * STRIDE
            return spare[0:rows, bass.ds(first, n * D)].rearrange("p (c n) -> p c n", c=n)
        mv = [small[:, 8 * u:8 * u + 8].rearrange("p (c k) -> p c k", k=2) for u in (0, 1)]
        std = [small[:, 16 + 4 * u:20 + 4 * u] for u in (0, 1)]
        rstd = [small[:, 24 + 4 * u:28 + 4 * u] for u in (0, 1)]
        shift = [small[:, 32 + 4 * u:36 + 4 * u] for u in (0, 1)]
        count = small[:, 40:42]
        vote = small[:, 42:43]
        ok = small[:, 43:44]
        ok_less_1 = small[:, 44:45]
        beyond = small[:, 45:46]
        bn_mv = small[:, 46:50].rearrange("p (h k) -> p h k", h=HALVES)
        bn_std = small[:, 50:52]
        bn_scale = small[:, 52:54]
        bn_shift = small[:, 54:56]
        stats6 = sb("stats6", [P, SUPER, 6])
        sn_row = sums[SUMS:SUMS + 1, 0:N]
        gen_rows = ring[:, 0, :]
        gen_sel = ring[:, 1:3, :].rearrange("p a n -> p (a n)")[:, 0:SUMS * P].rearrange("p (v n) -> p v n", v=SUMS)
        gen_nodes = ring[:, 3, 0:P]
        gen_rec = rec[:, 0, 0, :]

        bank = [ctx.enter_context(nc.psum_tensor(f"bank{k}", [P, 512], F32)) for k in range(8)]
        group_ps = [bank[0], bank[1]]
        def pick(v, rows):
            return ident[0:rows, v:v + 1].to_broadcast([rows, P])

        b_ps = bank[2][:, 0:HALVES * NB].rearrange("p (h n) -> p h n", h=HALVES)
        deg_bc = bank[3][:, 0:NB]
        abs_bc = bank[3][:, NB:2 * NB]
        w_bc = bank[4][:, 0:NB]
        inv_deg = bank[4][:, NB:2 * NB]
        inv_abs = bank[7][:, 0:NB]
        sn_bc = bank[6][:, 0:NB]
        out_ps = bank[5][:, 0:HALVES * NB].rearrange("p (h n) -> p h n", h=HALVES)
        t_ps = [bank[4 + p][:, :].rearrange("p (c h n) -> p c h n", c=2, h=HALVES) for p in (0, 1)]
        a_ps = [bank[6 + p][:, :].rearrange("p (c n) -> p c n", c=2) for p in (0, 1)]

        waits_carried = sem("waits_carried")
        small_loaded = sem("small_loaded")
        w_loaded = sem("w_loaded")
        edges_cleared = sem("edges_cleared")
        edges_loaded = sem("edges_loaded")
        consts = sem("consts")
        edges_float = sem("edges_float")
        edges_turned = sem("edges_turned")
        edges_copied = sem("edges_copied")
        base_spread = sem("base_spread")
        prep = sem("prep")
        voted = sem("voted")
        vote_sum = sem("vote_sum")
        recs_ready = sem("recs_ready")
        recs_stored = sem("recs_stored")
        flag_ready = sem("flag_ready")
        thresholds = sem("thresholds")
        zeroed = sem("zeroed")
        zeroed2 = sem("zeroed2")
        sums_zeroed = sem("sums_zeroed")
        x_loaded = sems("x_loaded", 2)
        ln_steps = sem("ln_steps")
        var_ready = sem("var_ready")
        std_ready = sem("std_ready")
        scale_ready = sem("scale_ready")
        h_ready = sems("h_ready", 2)
        xh_ready = sems("xh_ready", 2)
        h_turned = [sems(f"h_turned{u}_", 2) for u in (0, 1)]
        ht_copied = [sems(f"ht_copied{u}_", 2) for u in (0, 1)]
        ht_stored = sems("ht_stored", 2)
        ln_back = sems("ln_back", 2)
        fin_h_ready = sems("fin_h_ready", 2)
        a_done = [sems(f"a_done{u}_", 2) for u in (0, 1)]
        a_copied = [sems(f"a_copied{u}_", 2) for u in (0, 1)]
        a_stored = sems("a_stored", 2)
        gen_loaded = sem("gen_loaded")
        gen_gathered = sem("gen_gathered")
        gen_steps = sem("gen_steps")
        gen_sel_ready = sem("gen_sel_ready")
        gen_summed = sem("gen_summed")
        gen_added = sem("gen_added")
        rec_loaded = sems("rec_loaded", 2)
        gathered = sems("gathered", RING)
        sel_steps = sem("sel_steps")
        sel_ready = sem("sel_ready")
        passed = sem("passed")
        added = sem("added")
        blk_loaded = sem("blk_loaded")
        sn_loaded = sem("sn_loaded")
        bc_ready = sem("bc_ready")
        rows_ready = sem("rows_ready")
        b_done = sem("b_done")
        h_used = sem("h_used")
        b_ready = sem("b_ready")
        sn_ready = sem("sn_ready")
        blk_steps = sem("blk_steps")
        val_ready = sem("val_ready")
        diff_ready = sem("diff_ready")
        abs_ready = sem("abs_ready")
        out_done = sem("out_done")
        blk_done = sem("blk_done")
        bn_steps = sem("bn_steps")
        bn_var = sem("bn_var")
        bn_root = sem("bn_root")
        bn_ready = sem("bn_ready")
        fx_loaded = sem("fx_loaded")
        y_ready = sems("y_ready", 2)
        y_turned = sems("y_turned", 2)
        fin_ready = sems("fin_ready", 2)
        out_stored = sems("out_stored", 2)

        def super_rows(t, k, u, n=SUPER, rows=P):
            if n == 1:
                return t[full * P:full * P + rows, :].rearrange("(c p) n -> p c n", c=1)
            return t[bass.ds((2 * k + u) * (SUPER * P), SUPER * P), :].rearrange("(c p) n -> p c n", c=SUPER)

        def all_supers(engine, work):
            for u in (0, 1):
                work(0, u, SUPER, P)
            if pairs > 1:
                with engine.Fori(1, pairs) as k:
                    for u in (0, 1):
                        work(k, u, SUPER, P)
            work(pairs, 0, 1, tail_rows)

        def staggered(engine, first, second, after_first=None, after_second=None):
            first(0, 0, SUPER, P)
            first(0, 1, SUPER, P)
            if after_first:
                after_first()
            second(0, 0, SUPER, P)
            if after_second:
                after_second()
            if pairs > 1:
                first(1, 0, SUPER, P)
                second(0, 1, SUPER, P)
            if pairs > 2:
                with engine.Fori(1, pairs - 1) as k:
                    first(k, 1, SUPER, P)
                    second(k, 0, SUPER, P)
                    first(k + 1, 0, SUPER, P)
                    second(k, 1, SUPER, P)
            k = pairs - 1
            if pairs > 1:
                first(k, 1, SUPER, P)
                second(k, 0, SUPER, P)
            first(pairs, 0, 1, tail_rows)
            second(k, 1, SUPER, P)
            second(pairs, 0, 1, tail_rows)

        def before(u, k):
            return (0, k + 1) if u else (1, k)

        PARTS = 2 * GROUPS

        def edge_loop(engine, unit, part, before_last=None):
            def pair(k, first_block=False):
                for parity in (0, 1):
                    work = None
                    if not (isinstance(k, int) and k == 0):
                        def work(q, parity=parity):
                            if first_block:
                                part(parity * GROUPS + q, 0, 0, margin)
                            else:
                                part(parity * GROUPS + q, k - 1, (k - 1) * NB - margin, NB)
                    unit(2 * k + parity, parity, k, GROUPS, work)

            pair(0)
            pair(1, first_block=True)
            pair(2)
            with engine.Fori(3, unit_pairs) as k:
                pair(k)
            last_pair_done = 0
            tail = [(a, GROUPS) for a in range(2 * unit_pairs, units)] + [(units, rest)] * bool(rest)
            for a, n in tail:
                def work(q, parity=a % 2):
                    part(parity * GROUPS + q, unit_pairs - 1, (unit_pairs - 1) * NB - margin, NB)
                unit(a, a % 2, unit_pairs, n, work)
                last_pair_done += n
            for p in range(last_pair_done, PARTS):
                part(p, unit_pairs - 1, (unit_pairs - 1) * NB - margin, NB)
            if before_last:
                before_last()
            for p in range(PARTS):
                part(p, unit_pairs, unit_pairs * NB - margin, last_nb)

        def carry_waits(engine):
            engine.sem_inc(waits_carried, 1)

        def fast(engine):
            engine.wait_ge(flag_ready, 1)
            return engine.value_load(flag[0:1, 0:1], min_val=0, max_val=1)

        paired = unit_pairs * PARTS

        block = ctx.enter_context(nc.Block())

        @block.sync
        def _(sp):
            sp.wait_ge(edges_cleared, 3)
            for a, to in ((src, raw_i[0]), (dst, raw_i[1])):
                if full_rb:
                    sp.dma_start(to[:, 0:full_rb, :],
                                 a[0:full_rb * P * P].rearrange("(r t e) -> t r e", r=full_rb, t=P)).then_inc(edges_loaded, 16)
                if rest_rows:
                    sp.dma_start(to[0:rest_rows, full_rb, :],
                                 a[full_rb * P * P:(full_rb * P + rest_rows) * P].rearrange("(t e) -> t e", e=P)
                                 ).then_inc(edges_loaded, 16)
                if tail_edges:
                    sp.dma_start(to[rest_rows:rest_rows + 1, full_rb, 0:tail_edges],
                                 a[(full_rb * P + rest_rows) * P:E].rearrange("(t e) -> t e", t=1)).then_inc(edges_loaded, 16)
            if full_rb:
                sp.dma_start(eig_sb[:, 0:full_rb, :],
                             eig[0:full_rb * P * P, :].rearrange("(r t e) k -> t r (e k)", r=full_rb, t=P)
                             ).then_inc(edges_loaded, 16)
            if rest_rows:
                sp.dma_start(eig_sb[0:rest_rows, full_rb, :],
                             eig[full_rb * P * P:(full_rb * P + rest_rows) * P, :].rearrange("(t e) k -> t (e k)", e=P)
                             ).then_inc(edges_loaded, 16)
            if tail_edges:
                sp.dma_start(eig_sb[rest_rows:rest_rows + 1, full_rb, 0:2 * tail_edges],
                             eig[(full_rb * P + rest_rows) * P:E, :].rearrange("(t e) k -> t (e k)", t=1)
                             ).then_inc(edges_loaded, 16)

            def load_x(k, u, n, rows):
                if not (isinstance(k, int) and k == 0):
                    sp.wait_ge(h_ready[u], SUPER * k)
                    carry_waits(sp)
                sp.dma_start(x_sb[u][0:rows, 0:n, :], super_rows(x, k, u, n, rows)).then_inc(x_loaded[u], 16)

            all_supers(sp, load_x)
            sp.wait_ge(recs_stored, 16)

            with sp.If(fast(sp) == 0):
                with sp.Fori(0, rounds) as r:
                    with sp.Fori(0, slots) as t:
                        sp.wait_ge(gen_added, r * slots + t + 1)
                        sp.dma_start(gen_rec, rec_dram[:, bass.ds(t, 1), :].rearrange("p t k -> p (t k)")).then_inc(gen_loaded, 16)
                sp.wait_ge(gen_added, rounds * slots + 1)
            sp.nop()

            def unit(a, parity, pair, n, work):
                sp.wait_ge(passed, a * GROUPS)
                sp.dma_start(rec[:, parity, 0:n * TILES, :], rec_dram[:, bass.ds(a * UNIT, n * TILES), :]
                             ).then_inc(rec_loaded[parity], 16)
                if work and parity == 0:
                    work(0)

            def load_block(p, j, start, w):
                if p == 0:
                    if not (isinstance(j, int) and j == 0):
                        sp.wait_ge(diff_ready, j)
                        sp.wait_ge(h_used, j)
                    sp.dma_start(h_blk[:, :, 0:w], h_t_dram[:, :, bass.ds(start, w)].rearrange("h p n -> p h n")
                                 ).then_inc(blk_loaded, 16)

            def load_again(k, u, n, rows):
                sp.dma_start(fin_x(k, u, n, rows), super_rows(x, k, u, n, rows)).then_inc(fx_loaded, 16)

            def load_all_again():
                sp.wait_ge(blk_done, unit_pairs - 1)
                all_supers(sp, load_again)

            edge_loop(sp, unit, load_block, load_all_again if x_early else None)
            if not x_early:
                sp.wait_ge(blk_done, unit_pairs + 1)
                all_supers(sp, load_again)

            def store(k, u, n, rows):
                sp.wait_ge(fin_ready[u], k + 1)
                carry_waits(sp)
                sp.dma_start(super_rows(out, k, u, n, rows), fin_x(k, u, n, rows)).then_inc(out_stored[u], 16)

            all_supers(sp, store)
            sp.wait_ge(out_stored[0], 16 * (pairs + 1))
            sp.wait_ge(out_stored[1], 16 * pairs)

        @block.gpsimd
        def _(pool):
            pool.memset(raw_i[0][:, full_rb, :], 0).then_inc(edges_cleared, 1)
            pool.memset(raw_i[1][:, full_rb, :], -1).then_inc(edges_cleared, 1)
            pool.memset(eig_sb[:, full_rb, :], 0.0).then_inc(edges_cleared, 1)
            pool.memset(ident[:, :], 0.0).then_inc(consts, 1)
            pool.memset(ones[:, :], 1.0).then_inc(consts, 1)
            pool.memset(eps[:, :], LN_EPS).then_inc(consts, 1)
            pool.iota(iota_i[:, 0:WINDOW], [[1, WINDOW]], base=0, channel_multiplier=0).then_inc(consts, 1)
            pool.iota(thr_i[:, 0:paired], [[NB, unit_pairs], [0, PARTS]], base=-margin,
                      channel_multiplier=0).then_inc(thresholds, 1)
            if groups > paired:
                pool.iota(thr_i[:, paired:groups], [[0, groups - paired]], base=unit_pairs * NB - margin,
                          channel_multiplier=0).then_inc(thresholds, 1)
            pool.wait_ge(consts, 4)
            pool.affine_select(out=ident[:, :], in_=ident[:, :], compare_op=ALU.not_equal, fill=1.0, base=0,
                               pattern=[[-1, P]], channel_multiplier=1).then_inc(consts, 1)
            for v in range(SUMS):
                for h in range(HALVES):
                    if v * HALVES + h < 3:
                        pool.memset(table[:, v, h, :], 0.0).then_inc(zeroed, 1)

            def store_a(k, u, n, rows):
                for p in range(2 if n > 1 else 1):
                    pool.wait_ge(a_copied[u][p], k + 1)
                pool.dma_start(super_rows(a_dram, k, u, n, rows), a_sb[u][0:rows, 0:n, :]).then_inc(a_stored[u], 16)

            def store_recs():
                pool.wait_ge(recs_ready, 1)
                pool.dma_start(rec_dram, recs).then_inc(recs_stored, 16)

            def zero(p):
                pool.wait_ge(recs_ready, 1)
                pool.memset(plane[p], 0.0).then_inc(zeroed2, 1)

            store_a(0, 0, SUPER, P)
            store_a(0, 1, SUPER, P)
            store_recs()
            zero(3)
            if pairs > 1:
                store_a(1, 0, SUPER, P)
            zero(4)
            if pairs > 1:
                store_a(1, 1, SUPER, P)
            if pairs > 2:
                with pool.Fori(2, pairs) as k:
                    for u in (0, 1):
                        store_a(k, u, SUPER, P)
            store_a(pairs, 0, 1, tail_rows)

            pool.wait_ge(a_stored[0], 16 * (pairs + 1))
            pool.wait_ge(a_stored[1], 16 * pairs)
            with pool.If(fast(pool) == 0):
                with pool.Fori(0, rounds) as r:
                    with pool.Fori(0, slots) as t:
                        pool.wait_ge(gen_loaded, 16 * (r * slots + t + 1))
                        pool.wait_ge(gen_added, r * slots + t + 1)
                        carry_waits(pool)
                        pool.indirect_dma_start(
                            out=gen_rows, out_offset=None, in_=a_dram,
                            in_offset=bass.IndirectOffsetOnAxis(ap=gen_rec[:, SRC:SRC + 1].bitcast(U32), axis=0),
                        ).then_inc(gen_gathered, 16)
                pool.wait_ge(gen_added, rounds * slots + 1)
                pool.wait_ge(gen_steps, rounds * slots + rounds + 1)
            pool.nop()

            def unit(a, parity, pair, n, work):
                pool.wait_ge(rec_loaded[parity], 16 * (pair + 1))
                for q in range(n):
                    pool.wait_ge(passed, a * GROUPS + q + 1)
                    carry_waits(pool)
                    for t in range(TILES):
                        pool.indirect_dma_start(
                            out=ring[:, q * TILES + t, :], out_offset=None, in_=a_dram,
                            in_offset=bass.IndirectOffsetOnAxis(
                                ap=rec[:, parity, q * TILES + t, SRC:SRC + 1].bitcast(U32), axis=0),
                        ).then_inc(gathered[q], 16)

            edge_loop(pool, unit, lambda p, j, start, w: None)

            pool.wait_ge(fx_loaded, 16 * (supers + 1))

            def scale_again(k, u, n, rows):
                if not (isinstance(k, int) and k == 0):
                    pool.wait_ge(fin_h_ready[u], k)
                m = bass.ds((2 * k + u) * SUPER, n) if n > 1 else slice(full, full + 1)
                pool.tensor_copy(rstd[u][:, 0:n], ln_scale[:, m])
                pool.tensor_copy(shift[u][:, 0:n], ln_shift[:, m]).then_inc(ln_back[u], 1)

            def residual(k, u, n, rows):
                pool.wait_ge(fin_h_ready[u], k + 1)
                to = fin_x(k, u, n, rows)
                pool.tensor_tensor(to, to, fin_h[u][0:rows, 0:n, :], ALU.add).then_inc(xh_ready[u], 1)

            staggered(pool, scale_again, residual)

        @block.tensor
        def _(pe):
            pe.wait_ge(consts, 5)
            fill = 0
            for a in range(3):
                pe.wait_ge(edges_float, a + 1)
                for first in range(0, rows_in, 4):
                    if fill >= 4:
                        pe.wait_ge(edges_copied, fill - 3)
                    for r in range(first, min(first + 4, rows_in)):
                        rows = min(P, slots - r * P)
                        last = pe.transpose(bank[fill % 4][:, (r - first) * P:(r - first) * P + rows],
                                            raw_f[a][0:rows, r, :], ident[0:rows, 0:rows])
                    last.then_inc(edges_turned, 1)
                    fill += 1
            pe.wait_ge(edges_copied, fill)
            pe.matmul(bank[0][:, 0:groups], ones[0:1, :], recs[0:1, 0:slots:TILES, DST], start=True, stop=True
                      ).then_inc(base_spread, 1)

            def vote_matmul():
                pe.wait_ge(voted, 1)
                pe.matmul(bank[1][:, 0:1], ones[:, :], vote, start=True, stop=True).then_inc(vote_sum, 1)

            def turn(k, u, n, rows):
                for p in range(2 if n > 1 else 1):
                    pe.wait_ge(h_ready[u], SUPER * k + min(2 * p + 2, n))
                    b, done = before(u, k)
                    pe.wait_ge(ht_copied[b][p], done)
                    for c in range(min(2, n)):
                        for h in range(HALVES):
                            last = pe.transpose(t_ps[p][:, c, h, 0:rows], h_sb[u][0:rows, 2 * p + c, h * P:(h + 1) * P],
                                                ident[0:rows, 0:rows])
                    last.then_inc(h_turned[u][p], 1)

            def a_product(k, u, n, rows):
                for p in range(2 if n > 1 else 1):
                    pe.wait_ge(ht_copied[u][p], k + 1)
                    b, done = before(u, k)
                    pe.wait_ge(a_copied[b][p], done)
                    for c in range(min(2, n)):
                        m = (2 * p + c) * P
                        for h in range(HALVES):
                            last = pe.matmul(a_ps[p][0:rows, c, :], ht_sb[u][:, h, m:m + rows], w1a[:, h, :],
                                             start=(h == 0), stop=(h == HALVES - 1))
                    last.then_inc(a_done[u][p], 1)

            pe.wait_ge(w_loaded, 48)
            staggered(pe, turn, a_product, after_second=vote_matmul)

            with pe.If(fast(pe) == 0):
                with pe.Fori(0, rounds) as r:
                    with pe.Fori(0, slots) as t:
                        pe.wait_ge(gen_sel_ready, r * slots + t + 1)
                        pe.wait_ge(gen_gathered, 16 * (r * slots + t + 1))
                        for h in range(HALVES):
                            pe.matmul(bank[h][:, 0:SUMS * P], gen_rows[:, h * P:(h + 1) * P],
                                      gen_sel[:, :, :].rearrange("p v n -> p (v n)"), start=True, stop=True)
                        pe.matmul(bank[2][0:SUMS, 0:P], gen_rec[:, ONE:ONE + SUMS], gen_sel[:, 0, :],
                                  start=True, stop=True).then_inc(gen_summed, 1)
                pe.wait_ge(gen_added, rounds * slots + 1)
            pe.nop()
            pe.sem_inc(passed, RING)

            def sum_group(a, parity, q):
                g = a * GROUPS + q
                ps = group_ps[q % 2]
                pe.wait_ge(added, g)
                pe.wait_ge(sel_ready, g + 1)
                pe.wait_ge(gathered[q], 16 * TILES * (a + 1))
                for t in range(TILES):
                    for h in range(HALVES):
                        pe.matmul(ps[:, h * SEL:(h + 1) * SEL], ring[:, q * TILES + t, h * P:(h + 1) * P],
                                  sel[:, q % 2, t, :, :].rearrange("p v n -> p (v n)"),
                                  start=(t == 0 and h == 0), stop=(t == TILES - 1), skip_group_check=True)
                    last = pe.matmul(ps[0:SUMS, HALVES * SEL:HALVES * SEL + WINDOW],
                                     rec[:, parity, q * TILES + t, ONE:ONE + SUMS],
                                     sel[:, q % 2, t, 0, :], start=False, stop=(t == TILES - 1), skip_group_check=True)
                last.then_inc(passed, 1)

            def product(p, j, start, w):
                nodes = bass.ds(start, w)
                if p == 0:
                    pe.wait_ge(blk_loaded, 16 * j + 16)
                    if not (isinstance(j, int) and j == 0):
                        pe.wait_ge(b_ready, j)
                if p < 2:
                    for h in range(HALVES):
                        last = pe.matmul(b_ps[:, p, 0:w], w1b[:, h, p * P:(p + 1) * P], h_blk[:, h, 0:w],
                                         start=(h == 0), stop=(h == HALVES - 1), skip_group_check=True)
                if p == 1:
                    last.then_inc(b_done, 1)
                if p == 2:
                    pe.wait_ge(rows_ready, j + 1)
                    if not (isinstance(j, int) and j == 0):
                        pe.wait_ge(diff_ready, j)
                        pe.wait_ge(sn_ready, j)
                    for v, to in enumerate((deg_bc, abs_bc, w_bc)):
                        pe.matmul(to[:, 0:w], pick(v, SUMS), sums[0:SUMS, nodes], start=True, stop=True,
                                  skip_group_check=True)
                    for v, to in enumerate((inv_deg, inv_abs)):
                        pe.matmul(to[:, 0:w], pick(v, 2), inv_rows[:, 0:w], start=True, stop=True,
                                  skip_group_check=True)
                    pe.matmul(sn_bc[:, 0:w], pick(SUMS, SUMS + 1), sums[0:SUMS + 1, nodes], start=True, stop=True,
                              skip_group_check=True).then_inc(bc_ready, 1)
                inputs = [h_blk[:, :, 0:w]] + [table[:, v, :, nodes] for v in range(SUMS)]
                for i in range(*{2: (0, 2), 3: (2, 4), 4: (4, 7), 5: (7, 10), 6: (10, 13), 7: (13, 16)}.get(p, (0, 0))):
                    c, h, ho = i // 4, i // 2 % 2, i % 2
                    if i == 0 and not (isinstance(j, int) and j == 0):
                        pe.wait_ge(blk_done, j)
                    if i == 4:
                        pe.wait_ge(val_ready, 2 * j + 1)
                    if i == 8:
                        pe.wait_ge(val_ready, 2 * j + 2)
                    if i == 12:
                        pe.wait_ge(abs_ready, j + 1)
                    last = pe.matmul(out_ps[:, ho, 0:w], w2[:, c * HALVES + h, ho * P:(ho + 1) * P], inputs[c][:, h, :],
                                     start=(i == 0), stop=(i >= 14), skip_group_check=True)
                    if i == 3:
                        last.then_inc(h_used, 1)
                    if i == 15:
                        last.then_inc(out_done, 1)

            def unit(a, parity, pair, n, work):
                for q in range(n):
                    sum_group(a, parity, q)
                    if work:
                        work(q)

            pe.wait_ge(sn_loaded, 16)
            edge_loop(pe, unit, product)

            def turn_back(k, u, n, rows):
                pe.wait_ge(y_ready[u], k + 1)
                pe.wait_ge(fin_ready[u], k)
                for c in range(n):
                    for h in range(HALVES):
                        m = c * P if n > 1 else 0
                        last = pe.transpose(bank[2 * u + c // 2][0:rows, (c % 2) * D + h * P:(c % 2) * D + (h + 1) * P],
                                            fin_y[u][:, h, m:m + rows], ident[:, :])
                last.then_inc(y_turned[u], 1)

            all_supers(pe, turn_back)

        @block.scalar
        def _(act):
            for w, to in ((W1[0:D, :], w1a), (W1[D:2 * D, :], w1b[:, :, :]), (W2, w2[:, :, :])):
                act.dma_start(to, w.rearrange("(k p) n -> p k n", p=P)).then_inc(w_loaded, 16)
            for v, to in ((b1, b1_t), (b2, b2_t), (gamma, gamma_t), (beta, beta_t)):
                act.dma_start(to[:, :], v.rearrange("(h p) -> p h", p=P)).then_inc(small_loaded, 16)

            per_array = bool(full_rb) + bool(rest_rows) + bool(tail_edges)
            act.wait_ge(edges_loaded, 48 * per_array)
            for a in range(2):
                act.activation(raw_f[a], raw_i[a], ACT.Copy).then_inc(edges_float, 1)
            act.activation(raw_f[2], eig_sb[:, :, :].rearrange("p r (e k) -> p r e k", k=2)[:, :, :, 0], ACT.Copy
                           ).then_inc(edges_float, 1)
            fill = 0
            for word in (SRC, DST, ONE + 2):
                for first in range(0, rows_in, 4):
                    m = min(4 * P, slots - first * P)
                    act.wait_ge(edges_turned, fill + 1)
                    to = recs[:, first * P:first * P + m, word]
                    act.activation(to.bitcast(I32) if word == SRC else to, bank[fill % 4][:, 0:m], ACT.Copy
                                   ).then_inc(edges_copied, 1)
                    fill += 1

            def normal(k, u, n, rows):
                act.wait_ge(var_ready, 2 * k + u + 1)
                act.activation(std[u][0:rows, 0:n], mv[u][0:rows, 0:n, 1], ACT.Sqrt, bias=eps[0:rows, :]).then_inc(std_ready, 1)
                act.wait_ge(scale_ready, 2 * k + u + 1)
                act.wait_ge(h_turned[u][1], k)
                for c in range(n):
                    act.activation(h_sb[u][0:rows, c, :], x_sb[u][0:rows, c, :], ACT.Relu, bias=shift[u][0:rows, c:c + 1],
                                   scale=rstd[u][0:rows, c:c + 1]).then_inc(h_ready[u], 1)

            def keep(k, u, n, rows):
                m = min(2, n)
                halves = range(2 if n > 1 else 1)
                act.wait_ge(ht_stored[u], 16 * k)
                for p in halves:
                    act.wait_ge(h_turned[u][p], k + 1)
                    if n > 1:
                        to = ht_sb[u][:, :, 2 * p * P:(2 * p + 2) * P].rearrange("p h (c n) -> p c h n", c=2)
                        act.activation(to, t_ps[p], ACT.Copy).then_inc(ht_copied[u][p], 1)
                    else:
                        act.activation(ht_sb[u][:, :, 0:rows], t_ps[p][:, 0, :, 0:rows], ACT.Copy).then_inc(ht_copied[u][p], 1)
                for p in halves:
                    act.wait_ge(ht_copied[u][p], k + 1)
                carry_waits(act)
                if n > 1:
                    to = h_t_dram[:, :, bass.ds((2 * k + u) * (SUPER * P), n * P)]
                else:
                    to = h_t_dram[:, :, full * P:full * P + rows]
                act.dma_start(to.rearrange("h p n -> p h n"), ht_sb[u][:, :, 0:(n * P if n > 1 else rows)]
                              ).then_inc(ht_stored[u], 16)
                act.wait_ge(a_stored[u], 16 * k)
                for p in halves:
                    act.wait_ge(a_done[u][p], k + 1)
                    act.activation(a_sb[u][0:rows, 2 * p:2 * p + m, :], a_ps[p][0:rows, 0:m, :], ACT.Copy
                                   ).then_inc(a_copied[u][p], 1)

            act.wait_ge(consts, 5)
            staggered(act, normal, keep)
            act.wait_ge(zeroed, 3)
            for u in (0, 1):
                act.wait_ge(ht_stored[u], 16 * (pairs + 1 - u))
                act.wait_ge(a_done[u][0], pairs + 1 - u)
            act.activation(sums[0:SUMS, EARLY:NP], table[0:SUMS, 0, 0, EARLY:NP], ACT.Copy).then_inc(sums_zeroed, 1)
            act.wait_ge(sums_zeroed, 2)
            act.dma_start(sn_row, snorm.rearrange("n k -> k n")).then_inc(sn_loaded, 16)
            act.wait_ge(small_loaded, 64)

            def part(p, j, start, w):
                if p == 1:
                    act.wait_ge(b_done, j + 1)
                    if not (isinstance(j, int) and j == 0):
                        act.wait_ge(diff_ready, j)
                    for h in range(HALVES):
                        last = act.activation(b_rows[:, h, 0:w], b_ps[:, h, 0:w], ACT.Identity, bias=b1_t[:, h:h + 1])
                    last.then_inc(b_ready, 1)
                if p == 2:
                    if not (isinstance(j, int) and j == 0):
                        act.wait_ge(blk_done, j)
                    act.wait_ge(bc_ready, j + 1)
                    act.activation(sn[:, 0:w], sn_bc[:, 0:w], ACT.Copy).then_inc(sn_ready, 1)
                if p == 6:
                    act.wait_ge(diff_ready, j + 1)
                    diff = table[:, 2, :, bass.ds(start, w)]
                    act.activation(diff, diff, ACT.Abs).then_inc(abs_ready, 1)

            def unit(a, parity, pair, n, work):
                if work:
                    for q in range(n):
                        work(q)

            edge_loop(act, unit, part)

            def finish_stats():
                act.wait_ge(bn_var, 1)
                act.activation(bn_std, bn_mv[:, :, 1], ACT.Sqrt, bias=eps[:, :]).then_inc(bn_root, 1)
                act.wait_ge(bn_ready, 1)

            def normal_again(k, u, n, rows):
                act.wait_ge(ln_back[u], k + 1)
                if not (isinstance(k, int) and k == 0):
                    act.wait_ge(xh_ready[u], k)
                of = fin_x(k, u, n, rows)
                for c in range(n):
                    last = act.activation(fin_h[u][0:rows, c, :], of[:, c, :], ACT.Relu,
                                          bias=shift[u][0:rows, c:c + 1], scale=rstd[u][0:rows, c:c + 1])
                last.then_inc(fin_h_ready[u], 1)

            def activate(k, u, n, rows):
                act.wait_ge(y_turned[u], k)
                w = n * P if n > 1 else rows
                m = bass.ds((2 * k + u) * (SUPER * P), w) if n > 1 else bass.ds(full * P, w)
                for h in range(HALVES):
                    last = act.activation(fin_y[u][:, h, 0:w], table[:, 0, h, m], ACT.Relu, bias=bn_shift[:, h:h + 1],
                                          scale=bn_scale[:, h:h + 1])
                last.then_inc(y_ready[u], 1)

            act.wait_ge(fx_loaded, 16 * (supers + 1))
            staggered(act, normal_again, activate, finish_stats)

        @block.vector
        def _(dve):
            chained = [0]

            def link(ins):
                chained[0] += 1
                ins.then_inc(prep, 1)
                dve.wait_ge(prep, chained[0])

            rel = recs[:, :, REL]

            def take_records():
                dve.tensor_copy(nodes_iota[:, :], iota_i[:, 0:WINDOW])
                dve.memset(recs[:, :, ONE], 1.0)
                dve.wait_ge(edges_copied, 3 * (-(-rows_in // 4)))
                dve.scalar_tensor_tensor(out=recs[:, :, ONE + 1], in0=recs[:, :, ONE + 2], scalar=-1.0,
                                         in1=recs[:, :, ONE + 2], op0=ALU.mult, op1=ALU.max)
                dve.wait_ge(base_spread, 1)
                link(dve.tensor_tensor(recs[:, :, REL].rearrange("p (g t) -> p g t", t=TILES),
                                       recs[:, :, DST].rearrange("p (g t) -> p g t", t=TILES),
                                       bank[0][:, 0:groups].unsqueeze(2).to_broadcast([P, groups, TILES]), ALU.subtract))
                link(dve.tensor_single_scalar(mask[0], rel, 0.0, ALU.is_ge))
                link(dve.scalar_tensor_tensor(out=mask[1], in0=rel, scalar=float(WINDOW - 1), in1=mask[0],
                                              op0=ALU.is_le, op1=ALU.mult))
                link(dve.tensor_reduce(count[:, 0:1], mask[1], AX_X, ALU.add))

            def cast_votes():
                dve.wait_ge(thresholds, 2 if groups > paired else 1)
                link(dve.tensor_copy(mask[0][:, 0:groups], thr_i[:, 0:groups]))
                link(dve.tensor_tensor(mask[2][:, 0:groups], mask[0][:, 0:groups], bank[0][:, 0:groups], ALU.is_le))
                link(dve.tensor_reduce(count[:, 1:2], mask[2][:, 0:groups], AX_X, ALU.add))
                dve.tensor_tensor(vote, count[:, 0:1], count[:, 1:2], ALU.add).then_inc(voted, 1)

            def set_flag():
                dve.wait_ge(vote_sum, 1)
                link(dve.tensor_single_scalar(ok, bank[1][:, 0:1], float(E + P * groups), ALU.is_equal))
                dve.tensor_copy(flag[:, :], ok).then_inc(flag_ready, 1)
                link(dve.tensor_single_scalar(ok_less_1, ok, -1.0, ALU.add))
                link(dve.tensor_single_scalar(beyond, ok_less_1, float(-N), ALU.mult))
                base_f = recs[0:1, 0:slots:TILES, DST]
                dve.tensor_scalar(bases[:, 0:units, :], base_f[:, 0:units * GROUPS].rearrange("p (i q) -> p i q", q=GROUPS),
                                  ok[0:1, :], beyond[0:1, :], ALU.mult, ALU.add)
                if rest:
                    dve.tensor_scalar(bases[:, units, 0:rest], base_f[:, units * GROUPS:groups],
                                      ok[0:1, :], beyond[0:1, :], ALU.mult, ALU.add)
                dve.tensor_scalar(rel, rel, ok, ok_less_1, ALU.mult, ALU.add).then_inc(recs_ready, 1)

            def statistics(k, u, n, rows):
                s = 2 * k + u
                dve.wait_ge(x_loaded[u], 16 * (k + 1))
                for c in range(n):
                    last = dve.bn_stats(stats6[0:rows, c, :], x_sb[u][0:rows, c, :])
                last.then_inc(ln_steps, 1)
                dve.wait_ge(ln_steps, 2 * s + 1)
                carry_waits(dve)
                for c in range(n):
                    last = dve.bn_aggr(mv[u][0:rows, c, :], stats6[0:rows, c, :])
                last.then_inc(var_ready, 1)
                dve.wait_ge(std_ready, s + 1)
                dve.reciprocal(rstd[u][0:rows, 0:n], std[u][0:rows, 0:n]).then_inc(ln_steps, 1)
                dve.wait_ge(ln_steps, 2 * s + 2)
                dve.wait_ge(var_ready, s + 1)
                dve.scalar_tensor_tensor(out=shift[u][0:rows, 0:n], in0=mv[u][0:rows, 0:n, 0], scalar=-1.0,
                                         in1=rstd[u][0:rows, 0:n], op0=ALU.mult, op1=ALU.mult).then_inc(scale_ready, 1)
                m = bass.ds(s * SUPER, n) if n > 1 else slice(full, full + 1)
                dve.tensor_copy(ln_scale[0:rows, m], rstd[u][0:rows, 0:n])
                dve.wait_ge(scale_ready, s + 1)
                dve.tensor_copy(ln_shift[0:rows, m], shift[u][0:rows, 0:n])

            dve.wait_ge(consts, 5)
            dve.memset(ln_scale[:, :], 0.0)
            dve.memset(ln_shift[:, :], 0.0).then_inc(prep, 1)
            chained[0] += 1
            dve.wait_ge(prep, 1)
            statistics(0, 0, SUPER, P)
            statistics(0, 1, SUPER, P)
            take_records()
            if pairs > 1:
                statistics(1, 0, SUPER, P)
            cast_votes()
            if pairs > 1:
                statistics(1, 1, SUPER, P)
            set_flag()
            if pairs > 2:
                with dve.Fori(2, pairs) as k:
                    for u in (0, 1):
                        statistics(k, u, SUPER, P)
            statistics(pairs, 0, 1, tail_rows)
            dve.wait_ge(recs_stored, 16)
            dve.memset(plane[5], 0.0).then_inc(zeroed2, 1)

            for u in (0, 1):
                dve.wait_ge(ht_stored[u], 16 * (pairs + 1 - u))
                dve.wait_ge(a_done[u][0], pairs + 1 - u)
                dve.wait_ge(a_done[u][1], pairs)
            dve.memset(sums[0:SUMS, 0:EARLY], 0.0).then_inc(sums_zeroed, 1)
            dve.wait_ge(sums_zeroed, 2)
            dve.wait_ge(zeroed, 3)
            dve.wait_ge(zeroed2, 3)

            with dve.If(fast(dve) == 0):
                dve.sem_inc(gen_added, 1)
                for m in range(P // WINDOW):
                    last = dve.tensor_single_scalar(gen_nodes[:, m * WINDOW:(m + 1) * WINDOW], nodes_iota[:, :],
                                                    float(m * WINDOW), ALU.add)
                last.then_inc(gen_steps, 1)
                with dve.Fori(0, rounds) as r:
                    with dve.Fori(0, slots) as t:
                        n = r * slots + t
                        dve.wait_ge(gen_steps, n + r + 1)
                        dve.wait_ge(gen_loaded, 16 * (n + 1))
                        dve.tensor_scalar(gen_sel[:, 0, :], gen_nodes, gen_rec[:, DST:DST + 1], None, ALU.is_equal
                                          ).then_inc(gen_steps, 1)
                        dve.wait_ge(gen_steps, n + r + 2)
                        dve.tensor_scalar(gen_sel[:, 2, :], gen_sel[:, 0, :], gen_rec[:, ONE + 2:ONE + 3], None, ALU.mult)
                        dve.tensor_scalar(gen_sel[:, 1, :], gen_sel[:, 0, :], gen_rec[:, ONE + 1:ONE + 2], None, ALU.mult
                                          ).then_inc(gen_sel_ready, 1)
                        dve.wait_ge(gen_summed, n + 1)
                        nodes = bass.ds(r * P, P)
                        for h in range(HALVES):
                            dve.tensor_tensor(table[:, :, h, nodes], table[:, :, h, nodes],
                                              bank[h][:, 0:SUMS * P].rearrange("p (v n) -> p v n", v=SUMS), ALU.add)
                        dve.tensor_tensor(sums[0:SUMS, nodes], sums[0:SUMS, nodes], bank[2][0:SUMS, 0:P], ALU.add
                                          ).then_inc(gen_added, 1)
                        dve.wait_ge(gen_added, n + 2)
                    dve.tensor_single_scalar(gen_nodes, gen_nodes, float(P), ALU.add).then_inc(gen_steps, 1)
            dve.nop()
            dve.sem_inc(added, 1)
            base_regs = [[dve.alloc_register(f"base{u}_{q}") for q in range(GROUPS)] for u in (0, 1)]

            def window(parity, q):
                return dve.snap(base_regs[parity][q], min_val=0, max_val=N)

            def select(a, parity, pair, q):
                g = a * GROUPS + q
                if q == 0:
                    dve.wait_ge(rec_loaded[parity], 16 * (pair + 1))
                dve.wait_ge(passed, g + RING - 1)
                r = rec[:, parity, q * TILES:(q + 1) * TILES, :]
                s = sel[:, q % 2]
                dve.tensor_tensor(s[:, :, 0, :], nodes_iota[:, :].unsqueeze(1).to_broadcast([P, TILES, WINDOW]),
                                  r[:, :, REL:REL + 1].to_broadcast([P, TILES, WINDOW]), ALU.is_equal).then_inc(sel_steps, 1)
                dve.wait_ge(sel_steps, g + 1)
                dve.tensor_tensor(s[:, :, 1:SUMS, :], s[:, :, 0:1, :].to_broadcast([P, TILES, 2, WINDOW]),
                                  r[:, :, ONE + 1:ONE + 3].unsqueeze(3).to_broadcast([P, TILES, 2, WINDOW]),
                                  ALU.mult).then_inc(sel_ready, 1)

            def add(a, q, base):
                g = a * GROUPS + q
                ps = group_ps[q % 2]
                nodes = bass.ds(base, WINDOW)
                dve.wait_ge(passed, g + RING + 1)
                dve.wait_ge(added, g + 1)
                dve.tensor_tensor(table[:, :, :, nodes], table[:, :, :, nodes],
                                  ps[:, 0:HALVES * SEL].rearrange("p (h v n) -> p v h n", h=HALVES, v=SUMS), ALU.add)
                dve.tensor_tensor(sums[0:SUMS, nodes], sums[0:SUMS, nodes],
                                  ps[0:SUMS, HALVES * SEL:HALVES * SEL + WINDOW], ALU.add).then_inc(added, 1)

            STEPS = 9

            def step(j, n, ins):
                ins.then_inc(blk_steps, 1)
                dve.wait_ge(blk_steps, j * STEPS + n)

            def value(v, spread, inverse, j, n, nodes, w):
                to = table[:, v, :, nodes]
                step(j, n, dve.tensor_tensor(spread_b[:, :, 0:w], b_rows[:, :, 0:w],
                                             spread[:, 0:w].unsqueeze(1).to_broadcast([P, HALVES, w]), ALU.mult))
                step(j, n + 1, dve.tensor_tensor(to, to, spread_b[:, :, 0:w], ALU.add))
                return dve.tensor_tensor(to, to, inverse[:, 0:w].unsqueeze(1).to_broadcast([P, HALVES, w]), ALU.mult)

            def part(p, j, start, w):
                nodes = bass.ds(start, w)
                if p == 1:
                    dve.wait_ge(added, groups + 1 if isinstance(j, int) and j == unit_pairs else (j + 1) * PARTS + 1)
                    if not (isinstance(j, int) and j == 0):
                        dve.wait_ge(bc_ready, j)
                    step(j, 1, dve.tensor_scalar(inv_rows[:, 0:w], sums[0:2, nodes], ident[0:2, 0:1], abs_eps[:, :],
                                                 ALU.max, ALU.add))
                    dve.reciprocal(inv_rows[:, 0:w], inv_rows[:, 0:w]).then_inc(rows_ready, 1)
                if p == 3:
                    dve.wait_ge(bc_ready, j + 1)
                    dve.wait_ge(b_ready, j + 1)
                    value(0, deg_bc, inv_deg, j, 2, nodes, w).then_inc(val_ready, 1)
                if p == 4:
                    value(1, abs_bc, inv_abs, j, 4, nodes, w).then_inc(val_ready, 1)
                if p == 5:
                    step(j, 8, value(2, w_bc, inv_abs, j, 6, nodes, w))
                    diff = table[:, 2, :, nodes]
                    dve.tensor_tensor(diff, diff, h_blk[:, :, 0:w], ALU.subtract).then_inc(diff_ready, 1)
                if p == PARTS:
                    dve.wait_ge(out_done, j + 1)
                    dve.wait_ge(sn_ready, j + 1)
                    for h in range(HALVES):
                        last = dve.scalar_tensor_tensor(out=table[:, 0, h, nodes], in0=out_ps[:, h, 0:w],
                                                        scalar=b2_t[:, h:h + 1], in1=sn[:, 0:w], op0=ALU.add, op1=ALU.mult)
                    step(j, STEPS, last)
                    for h in range(HALVES):
                        last = dve.bn_stats(bn[:, h, bass.ds(j, 1), :].rearrange("p a k -> p (a k)"), table[:, 0, h, nodes])
                    last.then_inc(blk_done, 1)

            def part_and_finish(p, j, start, w):
                if p == 0 and not (isinstance(j, int) and j == 0):
                    if isinstance(j, int) and j == 1:
                        part(PARTS, 0, 0, margin)
                    else:
                        part(PARTS, j - 1, start - NB, NB)
                part(p, j, start, w)

            def unit(a, parity, pair, n, work):
                for q in range(n):
                    select(a, parity, pair, q)
                    if q:
                        add(a, q - 1, window(parity, q - 1))
                    else:
                        if not (isinstance(a, int) and a == 0):
                            add(a - 1, GROUPS - 1, window(1 - parity, GROUPS - 1))
                        dve.reg_load(base_regs[parity][0:n], bases[0:1, bass.ds(a, 1), 0:n].rearrange("p a k -> p (a k)"))
                    if work:
                        work(q)
                if isinstance(a, int) and a == (units if rest else units - 1):
                    add(a, n - 1, window(parity, n - 1))

            dve.wait_ge(small_loaded, 64)
            step_eps = dve.tensor_single_scalar(abs_eps[:, :], ident[0:2, 1:2], SUM_EPS, ALU.mult)
            step_eps.then_inc(bn_steps, 1)
            dve.wait_ge(bn_steps, 1)
            edge_loop(dve, unit, part_and_finish)
            part(PARTS, unit_pairs, unit_pairs * NB - margin, last_nb)

            chain = [1]

            def bn_link(ins):
                chain[0] += 1
                ins.then_inc(bn_steps, 1)
                dve.wait_ge(bn_steps, chain[0])

            dve.wait_ge(blk_done, unit_pairs + 1)
            for h in range(HALVES):
                last = dve.bn_aggr(bn_mv[:, h, :], bn[:, h, :, :].rearrange("p a k -> p (a k)"))
            last.then_inc(bn_var, 1)
            dve.wait_ge(bn_root, 1)
            bn_link(dve.reciprocal(bn_std, bn_std))
            bn_link(dve.tensor_tensor(bn_scale, bn_std, gamma_t[:, :], ALU.mult))
            bn_link(dve.tensor_tensor(bn_shift, bn_mv[:, :, 0], bn_scale, ALU.mult))
            dve.tensor_tensor(bn_shift, beta_t[:, :], bn_shift, ALU.subtract).then_inc(bn_ready, 1)

            def finish(k, u, n, rows):
                dve.wait_ge(xh_ready[u], k + 1)
                dve.wait_ge(y_turned[u], k + 1)
                for c in range(0, n, 2):
                    m = min(2, n)
                    to = fin_x(k, u, n, rows)[:, c:c + m, :]
                    last = dve.tensor_tensor(to, to, bank[2 * u + c // 2][0:rows, 0:m * D].rearrange("p (c n) -> p c n", c=m), ALU.add)
                last.then_inc(fin_ready[u], 1)

            all_supers(dve, finish)


_INS = ["x", "src", "dst", "edge_attr_2", "node_vec1", "L0_gnn_W1", "L0_gnn_b1", "L0_gnn_W2", "L0_gnn_b2",
        "L0_gnn_gamma", "L0_gnn_beta"]


def kernel(**inputs):
    import numpy as np
    import concourse.bacc as bacc
    from concourse.bass_utils import run_bass_kernel_spmd

    nc = bacc.Bacc("TRN2", target_bir_lowering=False, num_devices=1)
    arrays, args = {}, []
    for name in _INS:
        a = np.ascontiguousarray(inputs[name])
        arrays[f"in_{name}"] = a
        args.append(nc.dram_tensor(f"in_{name}", a.shape, mybir.dt.from_np(a.dtype), kind="ExternalInput").ap())
    out = nc.dram_tensor("out", inputs["x"].shape, F32, kind="ExternalOutput").ap()
    with nc.allow_non_contiguous_dma("four vectors of 256 features, one feature a partition"):
        build(nc, *args, out)
    r = run_bass_kernel_spmd(nc, [arrays], core_ids=[0])
    return r.results[0]["out"]
```

```python
from contextlib import ExitStack

import concourse.bass as bass
from concourse import mybir

F32 = mybir.dt.float32
I32 = mybir.dt.int32
U32 = mybir.dt.uint32
ALU = mybir.AluOpType
ACT = mybir.ActivationFunctionType
AX_X = mybir.AxisListType.X

P = 128
D = 256
HALVES = D // P
SUMS = 3
TILES = 3
WINDOW = 32
GROUPS = 4
RING = GROUPS
UNIT = GROUPS * TILES
WORDS = 6
SRC, DST, REL, ONE = 0, 1, 2, 3
SUPER = 4
SEL = SUMS * WINDOW
NORM_EPS = 1e-5
SUM_EPS = 1e-8


def build(nc, x, src, dst, eig, snorm, W1, b1, W2, b2, gamma, beta, out):
    N = x.shape[0]
    E = src.shape[0]
    tiles = -(-E // P)
    groups = -(-tiles // TILES)
    slots = groups * TILES
    units, rest = divmod(groups, GROUPS)
    margin = -(-N // units)
    NB = 2 * margin
    unit_pairs = units // 2
    PARTS = 2 * GROUPS
    last_nb = N - (unit_pairs * NB - margin)
    full, tail_rows = divmod(N, P)
    supers = full // SUPER
    pairs = supers // 2
    rounds = -(-N // P)
    tile_steps = 1 + 2 * rounds
    EARLY = 2048
    NP = -(-max(N + WINDOW, rounds * P, 6 * SUPER * D) // 16) * 16
    rows_in = -(-slots // P)
    full_rb, rest_rows = divmod(E // P, P)
    tail_edges = E % P
    assert full % (2 * SUPER) == 0 and pairs > 3 and 0 < tail_rows and unit_pairs > 4 and 0 < last_nb <= NB
    assert rows_in == full_rb + 1 and groups <= 512 and HALVES * NB <= 512 and slots * WORDS <= NP

    h_t_dram = nc.dram_tensor("h_t", [HALVES, P, (full + 1) * P], F32).ap()
    a_dram = nc.dram_tensor("a_rows", [N, D], F32).ap()
    xh_dram = nc.dram_tensor("x_plus_h", [N, D], F32).ap()
    rec_dram = nc.dram_tensor("edge_records", [P, slots, WORDS], F32).ap()

    ctx = ExitStack()
    with ctx:
        def sb(name, shape, dt=F32):
            return ctx.enter_context(nc.sbuf_tensor(name, shape, dt))

        def sem(name):
            return ctx.enter_context(nc.semaphore(name))

        def sems(name, n):
            return [sem(f"{name}{k}") for k in range(n)]

        table = sb("table", [P, SUMS, HALVES, NP])
        sums = sb("sums", [P, NP])
        ring = sb("ring", [P, RING * TILES, D])
        w1b = sb("w1b", [P, HALVES, D])
        w2 = sb("w2", [P, 4 * HALVES, D])
        ident = sb("ident", [P, P])
        ones = sb("ones", [P, P])
        nodes_iota = sb("nodes_iota", [P, WINDOW])
        eps = sb("eps", [P, 1])
        b1_t = sb("b1_t", [P, HALVES])
        b2_t = sb("b2_t", [P, HALVES])
        gamma_t = sb("gamma_t", [P, HALVES])
        beta_t = sb("beta_t", [P, HALVES])
        rec = sb("rec", [P, 2, UNIT, WORDS])
        sel = sb("sel", [P, 2, TILES, SUMS, WINDOW])
        b_rows = sb("b_rows", [P, HALVES, NB])
        h_blk = sb("h_blk", [P, HALVES, NB])
        spread_b = sb("spread_b", [P, HALVES, NB])
        inv_rows = sb("inv_rows", [2, NB])
        abs_eps = sb("abs_eps", [2, 1])
        sn = sb("sn", [P, NB])
        bn = sb("bn", [P, HALVES, unit_pairs + 1, 6])
        bases = sb("bases", [1, units + 1, GROUPS], I32)
        ln_scale = sb("ln_scale", [P, full + 1])
        ln_shift = sb("ln_shift", [P, full + 1])
        small = sb("small", [P, 64])
        flag = sb("flag", [P, 1], I32)

        lnb = sums[:, 0:6 * SUPER * D].rearrange("p (k c n) -> p k c n", k=6, c=SUPER)
        x_sb = [lnb[:, k] for k in (0, 1)]
        h_sb = [lnb[:, k] for k in (2, 3)]
        ht_sb = [lnb[:, k].rearrange("p c n -> p (c n)").rearrange("p (h n) -> p h n", h=HALVES) for k in (4, 5)]
        a_sb = [ring[:, SUPER * k:SUPER * k + SUPER, :] for k in (0, 1)]
        w1a = sel[:, :, :, :, :].rearrange("p a t v n -> p (a t v n)")[:, 0:HALVES * D].rearrange("p (h n) -> p h n", h=HALVES)
        plane = [table[:, v, h, :] for v in range(SUMS) for h in range(HALVES)]
        raw = plane[3]
        raw_n = rows_in * P
        raw_i = [raw[:, k * raw_n:(k + 1) * raw_n].bitcast(I32).rearrange("p (r e) -> p r e", r=rows_in) for k in (0, 1)]
        raw_f = [raw[:, k * raw_n:(k + 1) * raw_n].rearrange("p (r e) -> p r e", r=rows_in) for k in (2, 3, 4)]
        mask = [plane[4][:, k * slots:(k + 1) * slots] for k in range(3)]
        eig_sb = plane[4][:, 3 * slots:3 * slots + 2 * raw_n].rearrange("p (r e) -> p r e", r=rows_in)
        thr_i = plane[4][:, 3 * slots + 2 * raw_n:3 * slots + 2 * raw_n + groups].bitcast(I32)
        iota_i = plane[4][:, 3 * slots + 2 * raw_n + groups:3 * slots + 2 * raw_n + groups + WINDOW].bitcast(I32)
        assert 3 * slots + 2 * raw_n + groups + WINDOW <= NP and 5 * raw_n <= NP
        recs = plane[5][:, 0:slots * WORDS].rearrange("p (t k) -> p t k", k=WORDS)
        STRIDE = NP // 4
        spare = table[:, 1:SUMS, :, :].rearrange("p v h n -> p (v h n)")
        scratch = plane[5][:, D:D + 4 * SUPER * D].rearrange("p (k m) -> p k m", k=4)
        fin_h = [scratch[:, k].rearrange("p (c n) -> p c n", c=SUPER) for k in (0, 1)]
        fin_y = [scratch[:, k].rearrange("p (h n) -> p h n", h=HALVES) for k in (2, 3)]
        done_early = (unit_pairs - 1) * NB - margin
        x_early = done_early >= max(3 * STRIDE + SUPER * D, 5 * SUPER * D)

        def blocks_before_x(s):
            return -(-(s % 4 * STRIDE + SUPER * D + margin) // NB)

        x_at = {}
        for s in sorted(range(supers + 1), key=blocks_before_x):
            needs = blocks_before_x(s)
            first = 0 if needs <= unit_pairs - 3 else 6 if needs <= unit_pairs - 2 else PARTS + 2
            g = max([first] + [g + 1 for g in x_at])
            x_at[g + (g == PARTS + 3)] = s
        assert STRIDE >= SUPER * D and supers == 12 or supers < 12

        def fin_x(k, u, n, rows):
            first = (2 * k + u) * STRIDE
            return spare[0:rows, bass.ds(first, n * D)].rearrange("p (c n) -> p c n", c=n)
        mv = [small[:, 8 * u:8 * u + 8].rearrange("p (c k) -> p c k", k=2) for u in (0, 1)]
        std = [small[:, 16 + 4 * u:20 + 4 * u] for u in (0, 1)]
        rstd = [small[:, 24 + 4 * u:28 + 4 * u] for u in (0, 1)]
        shift = [small[:, 32 + 4 * u:36 + 4 * u] for u in (0, 1)]
        count = small[:, 40:42]
        vote = small[:, 42:43]
        ok = small[:, 43:44]
        ok_less_1 = small[:, 44:45]
        beyond = small[:, 45:46]
        bn_mv = small[:, 46:50].rearrange("p (h k) -> p h k", h=HALVES)
        bn_std = small[:, 50:52]
        bn_scale = small[:, 52:54]
        bn_shift = small[:, 54:56]
        stats6 = sb("stats6", [P, SUPER, 6])
        sn_row = sums[SUMS:SUMS + 1, 0:N]
        gen_rows = ring[:, 0, :]
        gen_sel = ring[:, 1:3, :].rearrange("p a n -> p (a n)")[:, 0:SUMS * P].rearrange("p (v n) -> p v n", v=SUMS)
        gen_nodes = ring[:, 3, 0:P]
        gen_rec = rec[:, 0, 0, :]

        bank = [ctx.enter_context(nc.psum_tensor(f"bank{k}", [P, 512], F32)) for k in range(8)]
        group_ps = [bank[0], bank[1]]
        def pick(v, rows):
            return ident[0:rows, v:v + 1].to_broadcast([rows, P])

        b_ps = bank[2][:, 0:HALVES * NB].rearrange("p (h n) -> p h n", h=HALVES)
        deg_bc = bank[3][:, 0:NB]
        abs_bc = bank[3][:, NB:2 * NB]
        w_bc = bank[4][:, 0:NB]
        inv_deg = bank[4][:, NB:2 * NB]
        inv_abs = bank[7][:, 0:NB]
        sn_bc = bank[6][:, 0:NB]
        out_ps = bank[5][:, 0:HALVES * NB].rearrange("p (h n) -> p h n", h=HALVES)
        t_ps = [bank[4 + p][:, :].rearrange("p (c h n) -> p c h n", c=2, h=HALVES) for p in (0, 1)]
        a_ps = [[bank[b + p][:, :].rearrange("p (c n) -> p c n", c=2) for p in (0, 1)] for b in (6, 2)]

        waits_carried = sem("waits_carried")
        small_loaded = sem("small_loaded")
        w1a_loaded = sem("w1a_loaded")
        w_loaded = sem("w_loaded")
        edges_cleared = sem("edges_cleared")
        edges_loaded = sem("edges_loaded")
        consts = sem("consts")
        edges_float = sem("edges_float")
        edges_turned = sem("edges_turned")
        edges_copied = sem("edges_copied")
        base_spread = sem("base_spread")
        prep = sem("prep")
        voted = sem("voted")
        vote_sum = sem("vote_sum")
        recs_ready = sem("recs_ready")
        recs_stored = sem("recs_stored")
        flag_ready = sem("flag_ready")
        thresholds = sem("thresholds")
        planes_zeroed = sem("planes_zeroed")
        edge_planes_zeroed = sem("edge_planes_zeroed")
        sums_zeroed = sem("sums_zeroed")
        x_loaded = sems("x_loaded", 2)
        ln_steps = sem("ln_steps")
        var_ready = sem("var_ready")
        std_ready = sem("std_ready")
        scale_ready = sem("scale_ready")
        h_ready = sems("h_ready", 2)
        xh_ready = sems("xh_ready", 2)
        h_turned = [sems(f"h_turned{u}_", 2) for u in (0, 1)]
        ht_copied = [sems(f"ht_copied{u}_", 2) for u in (0, 1)]
        ht_stored = sems("ht_stored", 2)
        ln_back = sems("ln_back", 2)
        fin_h_ready = sems("fin_h_ready", 2)
        a_done = [sems(f"a_done{u}_", 2) for u in (0, 1)]
        a_copied = [sems(f"a_copied{u}_", 2) for u in (0, 1)]
        a_stored = sems("a_stored", 2)
        gen_loaded = sem("gen_loaded")
        gen_gathered = sem("gen_gathered")
        gen_steps = sem("gen_steps")
        gen_sel_ready = sem("gen_sel_ready")
        gen_summed = sem("gen_summed")
        gen_added = sem("gen_added")
        rec_loaded = sems("rec_loaded", 2)
        gathered = sems("gathered", RING)
        sel_steps = sem("sel_steps")
        sel_ready = sem("sel_ready")
        passed = sem("passed")
        added = sem("added")
        blk_loaded = sem("blk_loaded")
        sn_loaded = sem("sn_loaded")
        bc_ready = sem("bc_ready")
        rows_ready = sem("rows_ready")
        b_done = sem("b_done")
        h_used = sem("h_used")
        b_ready = sem("b_ready")
        sn_ready = sem("sn_ready")
        blk_steps = sem("blk_steps")
        val_ready = sem("val_ready")
        diff_ready = sem("diff_ready")
        abs_ready = sem("abs_ready")
        out_done = sem("out_done")
        blk_done = sem("blk_done")
        bn_steps = sem("bn_steps")
        bn_var = sem("bn_var")
        bn_root = sem("bn_root")
        bn_ready = sem("bn_ready")
        fx_loaded = sem("fx_loaded")
        y_ready = sems("y_ready", 2)
        y_turned = sems("y_turned", 2)
        fin_ready = sems("fin_ready", 2)
        out_stored = sems("out_stored", 2)

        def super_rows(t, k, u, n=SUPER, rows=P):
            if n == 1:
                return t[full * P:full * P + rows, :].rearrange("(c p) n -> p c n", c=1)
            return t[bass.ds((2 * k + u) * (SUPER * P), SUPER * P), :].rearrange("(c p) n -> p c n", c=SUPER)

        def all_supers(engine, work, after_first=None):
            for u in (0, 1):
                work(0, u, SUPER, P)
            if after_first:
                after_first()
            with engine.Fori(1, pairs) as k:
                for u in (0, 1):
                    work(k, u, SUPER, P)
            work(pairs, 0, 1, tail_rows)

        def staggered(engine, first, second, after_first=None, after_second=None):
            first(0, 0, SUPER, P)
            first(0, 1, SUPER, P)
            if after_first:
                after_first()
            second(0, 0, SUPER, P)
            if after_second:
                after_second()
            first(1, 0, SUPER, P)
            second(0, 1, SUPER, P)
            with engine.Fori(1, pairs - 1) as k:
                first(k, 1, SUPER, P)
                second(k, 0, SUPER, P)
                first(k + 1, 0, SUPER, P)
                second(k, 1, SUPER, P)
            k = pairs - 1
            first(k, 1, SUPER, P)
            second(k, 0, SUPER, P)
            first(pairs, 0, 1, tail_rows)
            second(k, 1, SUPER, P)
            second(pairs, 0, 1, tail_rows)

        def before(u, k):
            return (0, k + 1) if u else (1, k)

        def edge_loop(engine, unit, part, before_last=None):
            def pair(k, first_block=False):
                for parity in (0, 1):
                    work = None
                    if not known(k, 0):
                        def work(q, parity=parity):
                            if first_block:
                                part(parity * GROUPS + q, 0, 0, margin)
                            else:
                                part(parity * GROUPS + q, k - 1, (k - 1) * NB - margin, NB)
                    unit(2 * k + parity, parity, k, GROUPS, work)

            pair(0)
            pair(1, first_block=True)
            pair(2)
            with engine.Fori(3, unit_pairs - 1) as k:
                pair(k)
            pair(unit_pairs - 1)
            parts_done = 0
            tail = [(a, GROUPS) for a in range(2 * unit_pairs, units)] + [(units, rest)] * bool(rest)
            for a, n in tail:
                def work(q, parity=a % 2):
                    part(parity * GROUPS + q, unit_pairs - 1, (unit_pairs - 1) * NB - margin, NB)
                unit(a, a % 2, unit_pairs, n, work)
                parts_done += n
            for p in range(parts_done, PARTS):
                part(p, unit_pairs - 1, (unit_pairs - 1) * NB - margin, NB)
            if before_last:
                before_last()
            for p in range(PARTS):
                part(p, unit_pairs, unit_pairs * NB - margin, last_nb)

        def known(number, *values):
            return isinstance(number, int) and number in values

        def carry_waits(engine):
            engine.sem_inc(waits_carried, 1)

        def fast(engine):
            engine.wait_ge(flag_ready, 1)
            return engine.value_load(flag[0:1, 0:1], min_val=0, max_val=1)

        paired = unit_pairs * PARTS

        block = ctx.enter_context(nc.Block())

        @block.sync
        def _(sp):
            def load_edges():
                sp.wait_ge(edges_cleared, 3)
                for a, to in ((src, raw_i[0]), (dst, raw_i[1])):
                    if full_rb:
                        sp.dma_start(to[:, 0:full_rb, :],
                                     a[0:full_rb * P * P].rearrange("(r t e) -> t r e", r=full_rb, t=P)).then_inc(edges_loaded, 16)
                    if rest_rows:
                        sp.dma_start(to[0:rest_rows, full_rb, :],
                                     a[full_rb * P * P:(full_rb * P + rest_rows) * P].rearrange("(t e) -> t e", e=P)
                                     ).then_inc(edges_loaded, 16)
                    if tail_edges:
                        sp.dma_start(to[rest_rows:rest_rows + 1, full_rb, 0:tail_edges],
                                     a[(full_rb * P + rest_rows) * P:E].rearrange("(t e) -> t e", t=1)).then_inc(edges_loaded, 16)
                if full_rb:
                    sp.dma_start(eig_sb[:, 0:full_rb, :],
                                 eig[0:full_rb * P * P, :].rearrange("(r t e) k -> t r (e k)", r=full_rb, t=P)
                                 ).then_inc(edges_loaded, 16)
                if rest_rows:
                    sp.dma_start(eig_sb[0:rest_rows, full_rb, :],
                                 eig[full_rb * P * P:(full_rb * P + rest_rows) * P, :].rearrange("(t e) k -> t (e k)", e=P)
                                 ).then_inc(edges_loaded, 16)
                if tail_edges:
                    sp.dma_start(eig_sb[rest_rows:rest_rows + 1, full_rb, 0:2 * tail_edges],
                                 eig[(full_rb * P + rest_rows) * P:E, :].rearrange("(t e) k -> t (e k)", t=1)
                                 ).then_inc(edges_loaded, 16)

            def load_x(k, u, n, rows):
                if not known(k, 0):
                    sp.wait_ge(h_ready[u], SUPER * k)
                    carry_waits(sp)
                sp.dma_start(x_sb[u][0:rows, 0:n, :], super_rows(x, k, u, n, rows)).then_inc(x_loaded[u], 16)

            all_supers(sp, load_x, load_edges)
            sp.wait_ge(recs_stored, 16)

            with sp.If(fast(sp) == 0):
                with sp.Fori(0, slots) as t:
                    sp.wait_ge(gen_added, t * rounds + 1)
                    sp.dma_start(gen_rec, rec_dram[:, bass.ds(t, 1), :].rearrange("p t k -> p (t k)")).then_inc(gen_loaded, 16)
                sp.wait_ge(gen_added, slots * rounds + 1)
            sp.nop()

            def unit(a, parity, pair, n, work):
                sp.wait_ge(passed, a * GROUPS)
                sp.dma_start(rec[:, parity, 0:n * TILES, :], rec_dram[:, bass.ds(a * UNIT, n * TILES), :]
                             ).then_inc(rec_loaded[parity], 16)
                if work:
                    for q in range(n):
                        work(q)

            def load_block(p, j, start, w):
                if p == 0:
                    if not known(j, 0):
                        sp.wait_ge(diff_ready, j)
                        sp.wait_ge(h_used, j)
                    sp.dma_start(h_blk[:, :, 0:w], h_t_dram[:, :, bass.ds(start, w)].rearrange("h p n -> p h n")
                                 ).then_inc(blk_loaded, 16)

            def load_again(s):
                k, u = divmod(s, 2)
                n, rows = (SUPER, P) if s < supers else (1, tail_rows)
                sp.dma_start(fin_x(k, u, n, rows), super_rows(x, k, u, n, rows)).then_inc(fx_loaded, 16)

            def load_part(p, j, start, w):
                load_block(p, j, start, w)
                if x_early and known(j, unit_pairs - 2, unit_pairs - 1):
                    g = (j - (unit_pairs - 2)) * PARTS + p
                    if g in x_at and g < groups - paired + PARTS:
                        s = x_at.pop(g)
                        sp.wait_ge(passed, paired - PARTS + g + 1)
                        sp.wait_ge(blk_done, blocks_before_x(s))
                        load_again(s)

            def load_rest():
                for s in x_at.values():
                    sp.wait_ge(blk_done, unit_pairs - 1 if x_early else unit_pairs + 1)
                    load_again(s)

            edge_loop(sp, unit, load_part, load_rest if x_early else None)
            if not x_early:
                load_rest()

            def store(k, u, n, rows):
                sp.wait_ge(fin_ready[u], k + 1)
                carry_waits(sp)
                sp.dma_start(super_rows(out, k, u, n, rows), fin_x(k, u, n, rows)).then_inc(out_stored[u], 16)

            all_supers(sp, store)
            sp.wait_ge(out_stored[0], 16 * (pairs + 1))
            sp.wait_ge(out_stored[1], 16 * pairs)

        @block.gpsimd
        def _(pool):
            pool.memset(raw_i[0][:, full_rb, :], 0).then_inc(edges_cleared, 1)
            pool.memset(raw_i[1][:, full_rb, :], -1).then_inc(edges_cleared, 1)
            pool.memset(eig_sb[:, full_rb, :], 0.0).then_inc(edges_cleared, 1)
            pool.memset(ident[:, :], 0.0).then_inc(consts, 1)
            pool.memset(ones[:, :], 1.0).then_inc(consts, 1)
            pool.memset(eps[:, :], NORM_EPS).then_inc(consts, 1)
            pool.iota(iota_i[:, 0:WINDOW], [[1, WINDOW]], base=0, channel_multiplier=0).then_inc(consts, 1)
            pool.iota(thr_i[:, 0:paired], [[NB, unit_pairs], [0, PARTS]], base=-margin,
                      channel_multiplier=0).then_inc(thresholds, 1)
            if groups > paired:
                pool.iota(thr_i[:, paired:groups], [[0, groups - paired]], base=unit_pairs * NB - margin,
                          channel_multiplier=0).then_inc(thresholds, 1)
            pool.wait_ge(consts, 4)
            pool.affine_select(out=ident[:, :], in_=ident[:, :], compare_op=ALU.not_equal, fill=1.0, base=0,
                               pattern=[[-1, P]], channel_multiplier=1).then_inc(consts, 1)
            for v in range(SUMS):
                for h in range(HALVES):
                    if v * HALVES + h < 3:
                        pool.memset(table[:, v, h, :], 0.0).then_inc(planes_zeroed, 1)

            def store_a(k, u, n, rows):
                for p in range(2 if n > 1 else 1):
                    pool.wait_ge(a_copied[u][p], k + 1)
                pool.dma_start(super_rows(a_dram, k, u, n, rows), a_sb[u][0:rows, 0:n, :]).then_inc(a_stored[u], 16)

            def store_recs():
                pool.wait_ge(recs_ready, 1)
                pool.dma_start(rec_dram, recs).then_inc(recs_stored, 16)

            def zero(p):
                pool.wait_ge(recs_ready, 1)
                pool.memset(plane[p], 0.0).then_inc(edge_planes_zeroed, 1)

            store_a(0, 0, SUPER, P)
            store_a(0, 1, SUPER, P)
            store_recs()
            zero(3)
            store_a(1, 0, SUPER, P)
            zero(4)
            store_a(1, 1, SUPER, P)
            pool.wait_ge(recs_stored, 16)
            zero(5)
            with pool.Fori(2, pairs) as k:
                for u in (0, 1):
                    store_a(k, u, SUPER, P)
            store_a(pairs, 0, 1, tail_rows)

            pool.wait_ge(a_stored[0], 16 * (pairs + 1))
            pool.wait_ge(a_stored[1], 16 * pairs)
            with pool.If(fast(pool) == 0):
                with pool.Fori(0, slots) as t:
                    pool.wait_ge(gen_loaded, 16 * (t + 1))
                    pool.wait_ge(gen_added, t * rounds + 1)
                    carry_waits(pool)
                    pool.indirect_dma_start(
                        out=gen_rows, out_offset=None, in_=a_dram,
                        in_offset=bass.IndirectOffsetOnAxis(ap=gen_rec[:, SRC:SRC + 1].bitcast(U32), axis=0),
                    ).then_inc(gen_gathered, 16)
                pool.wait_ge(gen_added, slots * rounds + 1)
                pool.wait_ge(gen_steps, slots * tile_steps)
            pool.nop()

            def unit(a, parity, pair, n, work):
                pool.wait_ge(rec_loaded[parity], 16 * (pair + 1))
                for q in range(n):
                    pool.wait_ge(passed, a * GROUPS + q + 1)
                    carry_waits(pool)
                    for t in range(TILES):
                        pool.indirect_dma_start(
                            out=ring[:, q * TILES + t, :], out_offset=None, in_=a_dram,
                            in_offset=bass.IndirectOffsetOnAxis(
                                ap=rec[:, parity, q * TILES + t, SRC:SRC + 1].bitcast(U32), axis=0),
                        ).then_inc(gathered[q], 16)

            edge_loop(pool, unit, lambda p, j, start, w: None)

            pool.wait_ge(fx_loaded, 16 * (supers + 1))

            def scale_again(k, u, n, rows):
                if not known(k, 0):
                    pool.wait_ge(fin_h_ready[u], k)
                m = bass.ds((2 * k + u) * SUPER, n) if n > 1 else slice(full, full + 1)
                pool.tensor_copy(rstd[u][:, 0:n], ln_scale[:, m])
                pool.tensor_copy(shift[u][:, 0:n], ln_shift[:, m]).then_inc(ln_back[u], 1)

            def residual(k, u, n, rows):
                pool.wait_ge(fin_h_ready[u], k + 1)
                to = fin_x(k, u, n, rows)
                pool.tensor_tensor(to, to, fin_h[u][0:rows, 0:n, :], ALU.add).then_inc(xh_ready[u], 1)

            staggered(pool, scale_again, residual)

        @block.tensor
        def _(pe):
            pe.wait_ge(consts, 5)

            def turn_edges():
                fill = 0
                for a in range(3):
                    pe.wait_ge(edges_float, a + 1)
                    for first in range(0, rows_in, 4):
                        if fill >= 4:
                            pe.wait_ge(edges_copied, fill - 3)
                        for r in range(first, min(first + 4, rows_in)):
                            rows = min(P, slots - r * P)
                            last = pe.transpose(bank[fill % 4][:, (r - first) * P:(r - first) * P + rows],
                                                raw_f[a][0:rows, r, :], ident[0:rows, 0:rows])
                        last.then_inc(edges_turned, 1)
                        fill += 1
                pe.wait_ge(edges_copied, fill)
                pe.matmul(bank[0][:, 0:groups], ones[0:1, :], recs[0:1, 0:slots:TILES, DST], start=True, stop=True
                          ).then_inc(base_spread, 1)

            def vote_matmul():
                pe.wait_ge(voted, 1)
                pe.matmul(bank[1][:, 0:1], ones[:, :], vote, start=True, stop=True).then_inc(vote_sum, 1)

            def turn(k, u, n, rows):
                for p in range(2 if n > 1 else 1):
                    pe.wait_ge(h_ready[u], SUPER * k + min(2 * p + 2, n))
                    b, done = before(u, k)
                    pe.wait_ge(ht_copied[b][p], done)
                    for c in range(min(2, n)):
                        for h in range(HALVES):
                            last = pe.transpose(t_ps[p][:, c, h, 0:rows], h_sb[u][0:rows, 2 * p + c, h * P:(h + 1) * P],
                                                ident[0:rows, 0:rows])
                    last.then_inc(h_turned[u][p], 1)

            def a_product(k, u, n, rows):
                for p in range(2 if n > 1 else 1):
                    pe.wait_ge(ht_copied[u][p], k + 1)
                    pe.wait_ge(a_copied[u][p], k)
                    for c in range(min(2, n)):
                        m = (2 * p + c) * P
                        for h in range(HALVES):
                            last = pe.matmul(a_ps[u][p][0:rows, c, :], ht_sb[u][:, h, m:m + rows], w1a[:, h, :],
                                             start=(h == 0), stop=(h == HALVES - 1))
                    last.then_inc(a_done[u][p], 1)
                if known(k, 0) and u == 1:
                    vote_matmul()

            pe.wait_ge(w1a_loaded, 16)
            staggered(pe, turn, a_product, after_first=turn_edges)

            pe.wait_ge(w_loaded, 32)
            with pe.If(fast(pe) == 0):
                with pe.Fori(0, slots) as t:
                    pe.wait_ge(gen_gathered, 16 * (t + 1))
                    carry_waits(pe)
                    with pe.Fori(0, rounds) as r:
                        pe.wait_ge(gen_sel_ready, t * rounds + r + 1)
                        for h in range(HALVES):
                            pe.matmul(bank[h][:, 0:SUMS * P], gen_rows[:, h * P:(h + 1) * P],
                                      gen_sel[:, :, :].rearrange("p v n -> p (v n)"), start=True, stop=True)
                        pe.matmul(bank[2][0:SUMS, 0:P], gen_rec[:, ONE:ONE + SUMS], gen_sel[:, 0, :],
                                  start=True, stop=True).then_inc(gen_summed, 1)
                pe.wait_ge(gen_added, slots * rounds + 1)
            pe.nop()
            pe.sem_inc(passed, RING)

            def sum_group(a, parity, q):
                g = a * GROUPS + q
                ps = group_ps[q % 2]
                pe.wait_ge(added, g)
                pe.wait_ge(sel_ready, g + 1)
                pe.wait_ge(gathered[q], 16 * TILES * (a + 1))
                for t in range(TILES):
                    for h in range(HALVES):
                        pe.matmul(ps[:, h * SEL:(h + 1) * SEL], ring[:, q * TILES + t, h * P:(h + 1) * P],
                                  sel[:, q % 2, t, :, :].rearrange("p v n -> p (v n)"),
                                  start=(t == 0 and h == 0), stop=(t == TILES - 1), skip_group_check=True)
                    last = pe.matmul(ps[0:SUMS, HALVES * SEL:HALVES * SEL + WINDOW],
                                     rec[:, parity, q * TILES + t, ONE:ONE + SUMS],
                                     sel[:, q % 2, t, 0, :], start=False, stop=(t == TILES - 1), skip_group_check=True)
                last.then_inc(passed, 1)

            def product(p, j, start, w):
                nodes = bass.ds(start, w)
                if p == 0:
                    pe.wait_ge(blk_loaded, 16 * j + 16)
                    if not known(j, 0):
                        pe.wait_ge(b_ready, j)
                if p < 2:
                    for h in range(HALVES):
                        last = pe.matmul(b_ps[:, p, 0:w], w1b[:, h, p * P:(p + 1) * P], h_blk[:, h, 0:w],
                                         start=(h == 0), stop=(h == HALVES - 1), skip_group_check=True)
                if p == 1:
                    last.then_inc(b_done, 1)
                if p == 2:
                    pe.wait_ge(rows_ready, j + 1)
                    if not known(j, 0):
                        pe.wait_ge(diff_ready, j)
                        pe.wait_ge(sn_ready, j)
                    for v, to in enumerate((deg_bc, abs_bc, w_bc)):
                        pe.matmul(to[:, 0:w], pick(v, SUMS), sums[0:SUMS, nodes], start=True, stop=True,
                                  skip_group_check=True)
                    for v, to in enumerate((inv_deg, inv_abs)):
                        pe.matmul(to[:, 0:w], pick(v, 2), inv_rows[:, 0:w], start=True, stop=True,
                                  skip_group_check=True)
                    pe.matmul(sn_bc[:, 0:w], pick(SUMS, SUMS + 1), sums[0:SUMS + 1, nodes], start=True, stop=True,
                              skip_group_check=True).then_inc(bc_ready, 1)
                inputs = [h_blk[:, :, 0:w]] + [table[:, v, :, nodes] for v in range(SUMS)]
                for i in range(*{2: (0, 2), 3: (2, 4), 4: (4, 7), 5: (7, 10), 6: (10, 13), 7: (13, 16)}.get(p, (0, 0))):
                    c, h, ho = i // 4, i // 2 % 2, i % 2
                    if i == 0 and not known(j, 0):
                        pe.wait_ge(blk_done, j)
                    if i == 4:
                        pe.wait_ge(val_ready, 2 * j + 1)
                    if i == 8:
                        pe.wait_ge(val_ready, 2 * j + 2)
                    if i == 12:
                        pe.wait_ge(abs_ready, j + 1)
                    last = pe.matmul(out_ps[:, ho, 0:w], w2[:, c * HALVES + h, ho * P:(ho + 1) * P], inputs[c][:, h, :],
                                     start=(i == 0), stop=(i >= 14), skip_group_check=True)
                    if i == 3:
                        last.then_inc(h_used, 1)
                    if i == 15:
                        last.then_inc(out_done, 1)

            def unit(a, parity, pair, n, work):
                for q in range(n):
                    sum_group(a, parity, q)
                    if work:
                        work(q)

            pe.wait_ge(sn_loaded, 16)
            edge_loop(pe, unit, product)

            def turn_back(k, u, n, rows):
                pe.wait_ge(y_ready[u], k + 1)
                pe.wait_ge(fin_ready[u], k)
                for c in range(n):
                    for h in range(HALVES):
                        m = c * P if n > 1 else 0
                        last = pe.transpose(bank[2 * u + c // 2][0:rows, (c % 2) * D + h * P:(c % 2) * D + (h + 1) * P],
                                            fin_y[u][:, h, m:m + rows], ident[:, :])
                last.then_inc(y_turned[u], 1)

            all_supers(pe, turn_back)

        @block.scalar
        def _(act):
            act.dma_start(w1a, W1[0:D, :].rearrange("(k p) n -> p k n", p=P)).then_inc(w1a_loaded, 16)

            def load_rest():
                for w, to in ((W1[D:2 * D, :], w1b), (W2, w2)):
                    act.dma_start(to[:, :, :], w.rearrange("(k p) n -> p k n", p=P)).then_inc(w_loaded, 16)
                for v, to in ((b1, b1_t), (b2, b2_t), (gamma, gamma_t), (beta, beta_t)):
                    act.dma_start(to[:, :], v.rearrange("(h p) -> p h", p=P)).then_inc(small_loaded, 16)

            def take_edges():
                per_array = bool(full_rb) + bool(rest_rows) + bool(tail_edges)
                act.wait_ge(edges_loaded, 48 * per_array)
                for a in range(2):
                    act.activation(raw_f[a], raw_i[a], ACT.Copy).then_inc(edges_float, 1)
                act.activation(raw_f[2], eig_sb[:, :, :].rearrange("p r (e k) -> p r e k", k=2)[:, :, :, 0], ACT.Copy
                               ).then_inc(edges_float, 1)
                fill = 0
                for word in (SRC, DST, ONE + 2):
                    for first in range(0, rows_in, 4):
                        m = min(4 * P, slots - first * P)
                        act.wait_ge(edges_turned, fill + 1)
                        to = recs[:, first * P:first * P + m, word]
                        act.activation(to.bitcast(I32) if word == SRC else to, bank[fill % 4][:, 0:m], ACT.Copy
                                       ).then_inc(edges_copied, 1)
                        fill += 1
                load_rest()

            def normal(k, u, n, rows):
                act.wait_ge(var_ready, 2 * k + u + 1)
                act.activation(std[u][0:rows, 0:n], mv[u][0:rows, 0:n, 1], ACT.Sqrt, bias=eps[0:rows, :]).then_inc(std_ready, 1)
                act.wait_ge(scale_ready, 2 * k + u + 1)
                act.wait_ge(h_turned[u][1], k)
                for c in range(n):
                    act.activation(h_sb[u][0:rows, c, :], x_sb[u][0:rows, c, :], ACT.Relu, bias=shift[u][0:rows, c:c + 1],
                                   scale=rstd[u][0:rows, c:c + 1]).then_inc(h_ready[u], 1)

            def keep(k, u, n, rows):
                halves = range(2 if n > 1 else 1)
                act.wait_ge(ht_stored[u], 16 * k)
                for p in halves:
                    act.wait_ge(h_turned[u][p], k + 1)
                    if n > 1:
                        to = ht_sb[u][:, :, 2 * p * P:(2 * p + 2) * P].rearrange("p h (c n) -> p c h n", c=2)
                        act.activation(to, t_ps[p], ACT.Copy).then_inc(ht_copied[u][p], 1)
                    else:
                        act.activation(ht_sb[u][:, :, 0:rows], t_ps[p][:, 0, :, 0:rows], ACT.Copy).then_inc(ht_copied[u][p], 1)
                for p in halves:
                    act.wait_ge(ht_copied[u][p], k + 1)
                carry_waits(act)
                if n > 1:
                    to = h_t_dram[:, :, bass.ds((2 * k + u) * (SUPER * P), n * P)]
                else:
                    to = h_t_dram[:, :, full * P:full * P + rows]
                act.dma_start(to.rearrange("h p n -> p h n"), ht_sb[u][:, :, 0:(n * P if n > 1 else rows)]
                              ).then_inc(ht_stored[u], 16)

            act.wait_ge(consts, 5)
            staggered(act, normal, keep, after_second=take_edges)
            act.wait_ge(planes_zeroed, 3)
            for u in (0, 1):
                act.wait_ge(ht_stored[u], 16 * (pairs + 1 - u))
                act.wait_ge(a_done[u][0], pairs + 1 - u)
            act.activation(sums[0:SUMS, EARLY:NP], table[0:SUMS, 0, 0, EARLY:NP], ACT.Copy).then_inc(sums_zeroed, 1)
            act.wait_ge(sums_zeroed, 2)
            act.dma_start(sn_row, snorm.rearrange("n k -> k n")).then_inc(sn_loaded, 16)
            act.wait_ge(small_loaded, 64)

            def normal_again(k, u, n, rows):
                act.wait_ge(ln_back[u], k + 1)
                if not known(k, 0):
                    act.wait_ge(xh_ready[u], k)
                of = fin_x(k, u, n, rows)
                for c in range(n):
                    last = act.activation(fin_h[u][0:rows, c, :], of[:, c, :], ACT.Relu,
                                          bias=shift[u][0:rows, c:c + 1], scale=rstd[u][0:rows, c:c + 1])
                last.then_inc(fin_h_ready[u], 1)

            h_again = {(unit_pairs - 1, 1): 2, (unit_pairs - 1, 3): 2, (unit_pairs - 1, 4): 2, (unit_pairs - 1, 7): 2,
                       (unit_pairs, 2): 2, (unit_pairs, 6): 1}
            left = list(range(supers + 1))

            def some_again(n):
                for s in left[0:n]:
                    if s == 0:
                        act.wait_ge(fx_loaded, 16 * (supers + 1))
                    if s < supers:
                        normal_again(s // 2, s % 2, SUPER, P)
                    else:
                        normal_again(pairs, 0, 1, tail_rows)
                del left[0:n]

            def part(p, j, start, w):
                block_part(p, j, start, w)
                if x_early and known(j, unit_pairs - 1, unit_pairs):
                    some_again(h_again.get((j, p), 0))

            def block_part(p, j, start, w):
                if p == 1:
                    act.wait_ge(b_done, j + 1)
                    if not known(j, 0):
                        act.wait_ge(diff_ready, j)
                    for h in range(HALVES):
                        last = act.activation(b_rows[:, h, 0:w], b_ps[:, h, 0:w], ACT.Identity, bias=b1_t[:, h:h + 1])
                    last.then_inc(b_ready, 1)
                if p == 2:
                    if not known(j, 0):
                        act.wait_ge(blk_done, j)
                    act.wait_ge(bc_ready, j + 1)
                    act.activation(sn[:, 0:w], sn_bc[:, 0:w], ACT.Copy).then_inc(sn_ready, 1)
                if p == 6:
                    act.wait_ge(diff_ready, j + 1)
                    diff = table[:, 2, :, bass.ds(start, w)]
                    act.activation(diff, diff, ACT.Abs).then_inc(abs_ready, 1)

            def unit(a, parity, pair, n, work):
                if work:
                    for q in range(n):
                        work(q)

            edge_loop(act, unit, part)

            def finish_stats():
                act.wait_ge(bn_var, 1)
                act.activation(bn_std, bn_mv[:, :, 1], ACT.Sqrt, bias=eps[:, :]).then_inc(bn_root, 1)
                act.wait_ge(bn_ready, 1)

            def activate(k, u, n, rows):
                act.wait_ge(y_turned[u], k)
                w = n * P if n > 1 else rows
                m = bass.ds((2 * k + u) * (SUPER * P), w) if n > 1 else bass.ds(full * P, w)
                for h in range(HALVES):
                    last = act.activation(fin_y[u][:, h, 0:w], table[:, 0, h, m], ACT.Relu, bias=bn_shift[:, h:h + 1],
                                          scale=bn_scale[:, h:h + 1])
                last.then_inc(y_ready[u], 1)

            some_again(0 if x_early else 2)
            finish_stats()
            activate(0, 0, SUPER, P)
            activate(0, 1, SUPER, P)
            some_again(len(left))
            with act.Fori(1, pairs) as k:
                for u in (0, 1):
                    activate(k, u, SUPER, P)
            activate(pairs, 0, 1, tail_rows)

        @block.vector
        def _(dve):
            chained = [0]

            def link(ins):
                chained[0] += 1
                ins.then_inc(prep, 1)
                dve.wait_ge(prep, chained[0])

            rel = recs[:, :, REL]

            def take_records():
                dve.tensor_copy(nodes_iota[:, :], iota_i[:, 0:WINDOW])
                dve.memset(recs[:, :, ONE], 1.0)
                dve.wait_ge(edges_copied, 3 * (-(-rows_in // 4)))
                dve.scalar_tensor_tensor(out=recs[:, :, ONE + 1], in0=recs[:, :, ONE + 2], scalar=-1.0,
                                         in1=recs[:, :, ONE + 2], op0=ALU.mult, op1=ALU.max)
                dve.wait_ge(base_spread, 1)
                link(dve.tensor_tensor(recs[:, :, REL].rearrange("p (g t) -> p g t", t=TILES),
                                       recs[:, :, DST].rearrange("p (g t) -> p g t", t=TILES),
                                       bank[0][:, 0:groups].unsqueeze(2).to_broadcast([P, groups, TILES]), ALU.subtract))

            def test_window():
                link(dve.tensor_single_scalar(mask[0], rel, 0.0, ALU.is_ge))
                link(dve.scalar_tensor_tensor(out=mask[1], in0=rel, scalar=float(WINDOW - 1), in1=mask[0],
                                              op0=ALU.is_le, op1=ALU.mult))
                link(dve.tensor_reduce(count[:, 0:1], mask[1], AX_X, ALU.add))

            def cast_votes():
                dve.wait_ge(thresholds, 2 if groups > paired else 1)
                link(dve.tensor_copy(mask[0][:, 0:groups], thr_i[:, 0:groups]))
                link(dve.tensor_tensor(mask[2][:, 0:groups], mask[0][:, 0:groups], bank[0][:, 0:groups], ALU.is_le))
                link(dve.tensor_reduce(count[:, 1:2], mask[2][:, 0:groups], AX_X, ALU.add))
                dve.tensor_tensor(vote, count[:, 0:1], count[:, 1:2], ALU.add).then_inc(voted, 1)

            def set_flag():
                dve.wait_ge(vote_sum, 1)
                link(dve.tensor_single_scalar(ok, bank[1][:, 0:1], float(E + P * groups), ALU.is_equal))
                dve.tensor_copy(flag[:, :], ok).then_inc(flag_ready, 1)
                link(dve.tensor_single_scalar(ok_less_1, ok, -1.0, ALU.add))
                link(dve.tensor_single_scalar(beyond, ok_less_1, float(-N), ALU.mult))
                base_f = recs[0:1, 0:slots:TILES, DST]
                dve.tensor_scalar(bases[:, 0:units, :], base_f[:, 0:units * GROUPS].rearrange("p (i q) -> p i q", q=GROUPS),
                                  ok[0:1, :], beyond[0:1, :], ALU.mult, ALU.add)
                if rest:
                    dve.tensor_scalar(bases[:, units, 0:rest], base_f[:, units * GROUPS:groups],
                                      ok[0:1, :], beyond[0:1, :], ALU.mult, ALU.add)
                dve.tensor_scalar(rel, rel, ok, ok_less_1, ALU.mult, ALU.add).then_inc(recs_ready, 1)

            def statistics(k, u, n, rows):
                s = 2 * k + u
                dve.wait_ge(x_loaded[u], 16 * (k + 1))
                for c in range(n):
                    last = dve.bn_stats(stats6[0:rows, c, :], x_sb[u][0:rows, c, :])
                last.then_inc(ln_steps, 1)
                dve.wait_ge(ln_steps, 2 * s + 1)
                carry_waits(dve)
                for c in range(n):
                    last = dve.bn_aggr(mv[u][0:rows, c, :], stats6[0:rows, c, :])
                last.then_inc(var_ready, 1)
                dve.wait_ge(std_ready, s + 1)
                dve.reciprocal(rstd[u][0:rows, 0:n], std[u][0:rows, 0:n]).then_inc(ln_steps, 1)
                dve.wait_ge(ln_steps, 2 * s + 2)
                dve.wait_ge(var_ready, s + 1)
                dve.scalar_tensor_tensor(out=shift[u][0:rows, 0:n], in0=mv[u][0:rows, 0:n, 0], scalar=-1.0,
                                         in1=rstd[u][0:rows, 0:n], op0=ALU.mult, op1=ALU.mult).then_inc(scale_ready, 1)
                m = bass.ds(s * SUPER, n) if n > 1 else slice(full, full + 1)
                dve.tensor_copy(ln_scale[0:rows, m], rstd[u][0:rows, 0:n])
                dve.wait_ge(scale_ready, s + 1)
                dve.tensor_copy(ln_shift[0:rows, m], shift[u][0:rows, 0:n])

            dve.wait_ge(consts, 5)
            dve.memset(ln_scale[:, :], 0.0)
            dve.memset(ln_shift[:, :], 0.0).then_inc(prep, 1)
            chained[0] += 1
            dve.wait_ge(prep, 1)
            def keep_a(k, u, n, rows):
                m = min(2, n)
                if not known(k, 0):
                    dve.wait_ge(a_stored[u], 16 * k)
                for p in range(2 if n > 1 else 1):
                    dve.wait_ge(a_done[u][p], k + 1)
                    dve.tensor_copy(a_sb[u][0:rows, 2 * p:2 * p + m, :], a_ps[u][p][0:rows, 0:m, :]).then_inc(a_copied[u][p], 1)

            statistics(0, 0, SUPER, P)
            statistics(0, 1, SUPER, P)
            statistics(1, 0, SUPER, P)
            take_records()
            keep_a(0, 0, SUPER, P)
            test_window()
            statistics(1, 1, SUPER, P)
            cast_votes()
            statistics(2, 0, SUPER, P)
            keep_a(0, 1, SUPER, P)
            set_flag()
            statistics(2, 1, SUPER, P)
            keep_a(1, 0, SUPER, P)
            with dve.Fori(3, pairs) as k:
                statistics(k, 0, SUPER, P)
                keep_a(k - 2, 1, SUPER, P)
                statistics(k, 1, SUPER, P)
                keep_a(k - 1, 0, SUPER, P)
            statistics(pairs, 0, 1, tail_rows)
            for k, u in ((pairs - 2, 1), (pairs - 1, 0), (pairs - 1, 1)):
                keep_a(k, u, SUPER, P)
            keep_a(pairs, 0, 1, tail_rows)

            for u in (0, 1):
                dve.wait_ge(ht_stored[u], 16 * (pairs + 1 - u))
                dve.wait_ge(a_done[u][0], pairs + 1 - u)
                dve.wait_ge(a_done[u][1], pairs)
            dve.memset(sums[0:SUMS, 0:EARLY], 0.0).then_inc(sums_zeroed, 1)
            dve.wait_ge(sums_zeroed, 2)
            dve.wait_ge(planes_zeroed, 3)
            dve.wait_ge(edge_planes_zeroed, 3)

            with dve.If(fast(dve) == 0):
                dve.sem_inc(gen_added, 1)
                with dve.Fori(0, slots) as t:
                    for m in range(P // WINDOW):
                        last = dve.tensor_single_scalar(gen_nodes[:, m * WINDOW:(m + 1) * WINDOW], nodes_iota[:, :],
                                                        float(m * WINDOW), ALU.add)
                    last.then_inc(gen_steps, 1)
                    dve.wait_ge(gen_loaded, 16 * (t + 1))
                    carry_waits(dve)
                    with dve.Fori(0, rounds) as r:
                        n = t * rounds + r
                        dve.wait_ge(gen_steps, t * tile_steps + 2 * r + 1)
                        dve.tensor_scalar(gen_sel[:, 0, :], gen_nodes, gen_rec[:, DST:DST + 1], None, ALU.is_equal
                                          ).then_inc(gen_steps, 1)
                        dve.wait_ge(gen_steps, t * tile_steps + 2 * r + 2)
                        dve.tensor_scalar(gen_sel[:, 2, :], gen_sel[:, 0, :], gen_rec[:, ONE + 2:ONE + 3], None, ALU.mult)
                        dve.tensor_scalar(gen_sel[:, 1, :], gen_sel[:, 0, :], gen_rec[:, ONE + 1:ONE + 2], None, ALU.mult
                                          ).then_inc(gen_sel_ready, 1)
                        dve.tensor_single_scalar(gen_nodes, gen_nodes, float(P), ALU.add).then_inc(gen_steps, 1)
                        dve.wait_ge(gen_summed, n + 1)
                        nodes = bass.ds(r * P, P)
                        for h in range(HALVES):
                            dve.tensor_tensor(table[:, :, h, nodes], table[:, :, h, nodes],
                                              bank[h][:, 0:SUMS * P].rearrange("p (v n) -> p v n", v=SUMS), ALU.add)
                        dve.tensor_tensor(sums[0:SUMS, nodes], sums[0:SUMS, nodes], bank[2][0:SUMS, 0:P], ALU.add
                                          ).then_inc(gen_added, 1)
                        dve.wait_ge(gen_added, n + 2)
            dve.nop()
            dve.sem_inc(added, 1)
            base_regs = [[dve.alloc_register(f"base{u}_{q}") for q in range(GROUPS)] for u in (0, 1)]

            def window(parity, q):
                return dve.snap(base_regs[parity][q], min_val=0, max_val=N)

            def select(a, parity, pair, q):
                g = a * GROUPS + q
                if q == 0:
                    dve.wait_ge(rec_loaded[parity], 16 * (pair + 1))
                dve.wait_ge(passed, g + RING - 1)
                r = rec[:, parity, q * TILES:(q + 1) * TILES, :]
                s = sel[:, q % 2]
                dve.tensor_tensor(s[:, :, 0, :], nodes_iota[:, :].unsqueeze(1).to_broadcast([P, TILES, WINDOW]),
                                  r[:, :, REL:REL + 1].to_broadcast([P, TILES, WINDOW]), ALU.is_equal).then_inc(sel_steps, 1)
                dve.wait_ge(sel_steps, g + 1)
                dve.tensor_tensor(s[:, :, 1:SUMS, :], s[:, :, 0:1, :].to_broadcast([P, TILES, 2, WINDOW]),
                                  r[:, :, ONE + 1:ONE + 3].unsqueeze(3).to_broadcast([P, TILES, 2, WINDOW]),
                                  ALU.mult).then_inc(sel_ready, 1)

            def add(a, q, base):
                g = a * GROUPS + q
                ps = group_ps[q % 2]
                nodes = bass.ds(base, WINDOW)
                dve.wait_ge(passed, g + RING + 1)
                dve.wait_ge(added, g + 1)
                dve.tensor_tensor(table[:, :, :, nodes], table[:, :, :, nodes],
                                  ps[:, 0:HALVES * SEL].rearrange("p (h v n) -> p v h n", h=HALVES, v=SUMS), ALU.add)
                dve.tensor_tensor(sums[0:SUMS, nodes], sums[0:SUMS, nodes],
                                  ps[0:SUMS, HALVES * SEL:HALVES * SEL + WINDOW], ALU.add).then_inc(added, 1)

            STEPS = 9

            def step(j, n, ins):
                ins.then_inc(blk_steps, 1)
                dve.wait_ge(blk_steps, j * STEPS + n)

            def value(v, spread, inverse, j, n, nodes, w):
                to = table[:, v, :, nodes]
                step(j, n, dve.tensor_tensor(spread_b[:, :, 0:w], b_rows[:, :, 0:w],
                                             spread[:, 0:w].unsqueeze(1).to_broadcast([P, HALVES, w]), ALU.mult))
                step(j, n + 1, dve.tensor_tensor(to, to, spread_b[:, :, 0:w], ALU.add))
                return dve.tensor_tensor(to, to, inverse[:, 0:w].unsqueeze(1).to_broadcast([P, HALVES, w]), ALU.mult)

            def part(p, j, start, w):
                nodes = bass.ds(start, w)
                if p == 1:
                    dve.wait_ge(added, groups + 1 if known(j, unit_pairs) else (j + 1) * PARTS + 1)
                    if not known(j, 0):
                        dve.wait_ge(bc_ready, j)
                    step(j, 1, dve.tensor_scalar(inv_rows[:, 0:w], sums[0:2, nodes], ident[0:2, 0:1], abs_eps[:, :],
                                                 ALU.max, ALU.add))
                    dve.reciprocal(inv_rows[:, 0:w], inv_rows[:, 0:w]).then_inc(rows_ready, 1)
                if p == 3:
                    dve.wait_ge(bc_ready, j + 1)
                    dve.wait_ge(b_ready, j + 1)
                    value(0, deg_bc, inv_deg, j, 2, nodes, w).then_inc(val_ready, 1)
                if p == 4:
                    value(1, abs_bc, inv_abs, j, 4, nodes, w).then_inc(val_ready, 1)
                if p == 5:
                    step(j, 8, value(2, w_bc, inv_abs, j, 6, nodes, w))
                    diff = table[:, 2, :, nodes]
                    dve.tensor_tensor(diff, diff, h_blk[:, :, 0:w], ALU.subtract).then_inc(diff_ready, 1)
                if p == PARTS:
                    dve.wait_ge(out_done, j + 1)
                    dve.wait_ge(sn_ready, j + 1)
                    for h in range(HALVES):
                        last = dve.scalar_tensor_tensor(out=table[:, 0, h, nodes], in0=out_ps[:, h, 0:w],
                                                        scalar=b2_t[:, h:h + 1], in1=sn[:, 0:w], op0=ALU.add, op1=ALU.mult)
                    step(j, STEPS, last)
                    for h in range(HALVES):
                        last = dve.bn_stats(bn[:, h, bass.ds(j, 1), :].rearrange("p a k -> p (a k)"), table[:, 0, h, nodes])
                    last.then_inc(blk_done, 1)

            def part_and_finish(p, j, start, w):
                if p == 0 and not known(j, 0):
                    if known(j, 1):
                        part(PARTS, 0, 0, margin)
                    else:
                        part(PARTS, j - 1, start - NB, NB)
                part(p, j, start, w)

            def unit(a, parity, pair, n, work):
                for q in range(n):
                    select(a, parity, pair, q)
                    if q:
                        add(a, q - 1, window(parity, q - 1))
                    else:
                        if not known(a, 0):
                            add(a - 1, GROUPS - 1, window(1 - parity, GROUPS - 1))
                        dve.reg_load(base_regs[parity][0:n], bases[0:1, bass.ds(a, 1), 0:n].rearrange("p a k -> p (a k)"))
                    if work:
                        work(q)
                if known(a, (units if rest else units - 1)):
                    add(a, n - 1, window(parity, n - 1))

            dve.wait_ge(small_loaded, 64)
            dve.tensor_single_scalar(abs_eps[:, :], ident[0:2, 1:2], SUM_EPS, ALU.mult).then_inc(bn_steps, 1)
            dve.wait_ge(bn_steps, 1)
            edge_loop(dve, unit, part_and_finish)
            part(PARTS, unit_pairs, unit_pairs * NB - margin, last_nb)

            chain = [1]

            def bn_link(ins):
                chain[0] += 1
                ins.then_inc(bn_steps, 1)
                dve.wait_ge(bn_steps, chain[0])

            dve.wait_ge(blk_done, unit_pairs + 1)
            for h in range(HALVES):
                last = dve.bn_aggr(bn_mv[:, h, :], bn[:, h, :, :].rearrange("p a k -> p (a k)"))
            last.then_inc(bn_var, 1)
            dve.wait_ge(bn_root, 1)
            bn_link(dve.reciprocal(bn_std, bn_std))
            bn_link(dve.tensor_tensor(bn_scale, bn_std, gamma_t[:, :], ALU.mult))
            bn_link(dve.tensor_tensor(bn_shift, bn_mv[:, :, 0], bn_scale, ALU.mult))
            dve.tensor_tensor(bn_shift, beta_t[:, :], bn_shift, ALU.subtract).then_inc(bn_ready, 1)

            def finish(k, u, n, rows):
                dve.wait_ge(xh_ready[u], k + 1)
                dve.wait_ge(y_turned[u], k + 1)
                for c in range(0, n, 2):
                    m = min(2, n)
                    to = fin_x(k, u, n, rows)[:, c:c + m, :]
                    last = dve.tensor_tensor(to, to, bank[2 * u + c // 2][0:rows, 0:m * D].rearrange("p (c n) -> p c n", c=m), ALU.add)
                last.then_inc(fin_ready[u], 1)

            all_supers(dve, finish)


_INS = ["x", "src", "dst", "edge_attr_2", "node_vec1", "L0_gnn_W1", "L0_gnn_b1", "L0_gnn_W2", "L0_gnn_b2",
        "L0_gnn_gamma", "L0_gnn_beta"]


def kernel(**inputs):
    import numpy as np
    import concourse.bacc as bacc
    from concourse.bass_utils import run_bass_kernel_spmd

    nc = bacc.Bacc("TRN2", target_bir_lowering=False, num_devices=1)
    arrays, args = {}, []
    for name in _INS:
        a = np.ascontiguousarray(inputs[name])
        arrays[f"in_{name}"] = a
        args.append(nc.dram_tensor(f"in_{name}", a.shape, mybir.dt.from_np(a.dtype), kind="ExternalInput").ap())
    out = nc.dram_tensor("out", inputs["x"].shape, F32, kind="ExternalOutput").ap()
    with nc.allow_non_contiguous_dma("four vectors of 256 features, one feature a partition"):
        build(nc, *args, out)
    r = run_bass_kernel_spmd(nc, [arrays], core_ids=[0])
    return r.results[0]["out"]
```
